# Optimizing a Trainium2 kernel written in Bass

```python
import numpy as np
import jax
import jax.numpy as jnp

def _softmax(x, axis=-1):
    return jax.nn.softmax(x, axis=axis)
def _gelu(x):
    return jax.nn.gelu(x, approximate=True)
def _silu(x):
    return jax.nn.silu(x)
def _sigmoid(x):
    return jax.nn.sigmoid(x)
def _layernorm(x, axis=-1, eps=1e-5):
    m = jnp.mean(x, axis=axis, keepdims=True)
    v = jnp.var(x, axis=axis, keepdims=True)
    return (x - m) / jnp.sqrt(v + eps)
def _scatter_add(tgt, idx, src, axis=0):
    return tgt.at[idx].add(src)
def _segment_sum(src, seg, n):
    return jax.ops.segment_sum(src, seg, n)

kernel_name = 'mk_conv_seq_d1_conv_nchw128_f49940'

def setup_inputs(seed: int = 0):
    np.random.seed(seed)
    _w = jnp.asarray
    def _rec_inputs():
        import jax
        import jax.numpy as jnp
        _gk = jax.random.key(seed)
        x = -8.015e-05 + 0.9999 * jax.random.normal(jax.random.fold_in(_gk, 1), (16, 128, 160, 160), jnp.float32)
        return x
    x = _rec_inputs()
    def _L0_conv_setup():
        import jax, jax.numpy as jnp
        import numpy as np
        B, C, H, W = (16, 128, 160, 160)
        C2 = C // 2
        KS1 = [3, 5]
        KS2 = [7, 9, 11]
        DIL2 = 3

        def _dwconv(x, w, b, dilation):
            k = w.shape[-1]
            pad = dilation * (k // 2)
            y = jax.lax.conv_general_dilated(x, w, window_strides=(1, 1), padding=[(pad, pad), (pad, pad)], rhs_dilation=(dilation, dilation), dimension_numbers=('NCHW', 'OIHW', 'NCHW'), feature_group_count=x.shape[1])
            return y + b[None, :, None, None]

        def _route(x, att_w, att_b, conv_ws, conv_bs, dilation):
            pooled = x.mean(axis=(2, 3))
            logits = pooled @ att_w.T + att_b
            weights = jax.nn.softmax(logits, axis=1)
            idx = jnp.argmax(weights, axis=1)
            outs = jnp.stack([_dwconv(x, w, b, dilation) for w, b in zip(conv_ws, conv_bs)], axis=1)
            sel = jnp.take_along_axis(outs, idx[:, None, None, None, None], axis=1)[:, 0]
            return sel
        key = jax.random.key(seed)
        ks = jax.random.split(key, 20)
        s = 0.05
        inp = {'x': jax.random.normal(ks[0], (B, C, H, W), jnp.float32)}
        inp['proj_w'] = jax.random.normal(ks[1], (C2, C), jnp.float32) * s
        for i, k in enumerate(KS1):
            inp[f'dw1_w{k}'] = jax.random.normal(ks[2 + i], (C2, 1, k, k), jnp.float32) * s
            inp[f'dw1_b{k}'] = jnp.zeros((C2,), jnp.float32)
        for i, k in enumerate(KS2):
            inp[f'dw2_w{k}'] = jax.random.normal(ks[5 + i], (C2, 1, k, k), jnp.float32) * s
            inp[f'dw2_b{k}'] = jnp.zeros((C2,), jnp.float32)
        inp['att1_w'] = jax.random.normal(ks[9], (len(KS1), C2), jnp.float32) * s
        inp['att1_b'] = jnp.zeros((len(KS1),), jnp.float32)
        inp['att2_w'] = jax.random.normal(ks[10], (len(KS2), C2), jnp.float32) * s
        inp['att2_b'] = jnp.zeros((len(KS2),), jnp.float32)
        inp['sp_w'] = jax.random.normal(ks[11], (2, 2, 7, 7), jnp.float32) * s
        inp['sp_b'] = jnp.zeros((2,), jnp.float32)
        return inp
    _L0_conv_all = _L0_conv_setup()
    _L0_conv_in = {k: v for k, v in _L0_conv_all.items() if k in ('proj_w', 'dw1_w3', 'dw1_b3', 'dw1_w5', 'dw1_b5', 'dw2_w7', 'dw2_b7', 'dw2_w9', 'dw2_b9', 'dw2_w11', 'dw2_b11', 'att1_w', 'att1_b', 'att2_w', 'att2_b', 'sp_w', 'sp_b', )}
    del _L0_conv_all

    return {
        "x": x,
        "L0_conv_proj_w": _L0_conv_in["proj_w"],
        "L0_conv_dw1_w3": _L0_conv_in["dw1_w3"],
        "L0_conv_dw1_b3": _L0_conv_in["dw1_b3"],
        "L0_conv_dw1_w5": _L0_conv_in["dw1_w5"],
        "L0_conv_dw1_b5": _L0_conv_in["dw1_b5"],
        "L0_conv_dw2_w7": _L0_conv_in["dw2_w7"],
        "L0_conv_dw2_b7": _L0_conv_in["dw2_b7"],
        "L0_conv_dw2_w9": _L0_conv_in["dw2_w9"],
        "L0_conv_dw2_b9": _L0_conv_in["dw2_b9"],
        "L0_conv_dw2_w11": _L0_conv_in["dw2_w11"],
        "L0_conv_dw2_b11": _L0_conv_in["dw2_b11"],
        "L0_conv_att1_w": _L0_conv_in["att1_w"],
        "L0_conv_att1_b": _L0_conv_in["att1_b"],
        "L0_conv_att2_w": _L0_conv_in["att2_w"],
        "L0_conv_att2_b": _L0_conv_in["att2_b"],
        "L0_conv_sp_w": _L0_conv_in["sp_w"],
        "L0_conv_sp_b": _L0_conv_in["sp_b"],
    }

def reference(x, L0_conv_proj_w, L0_conv_dw1_w3, L0_conv_dw1_b3, L0_conv_dw1_w5, L0_conv_dw1_b5, L0_conv_dw2_w7, L0_conv_dw2_b7, L0_conv_dw2_w9, L0_conv_dw2_b9, L0_conv_dw2_w11, L0_conv_dw2_b11, L0_conv_att1_w, L0_conv_att1_b, L0_conv_att2_w, L0_conv_att2_b, L0_conv_sp_w, L0_conv_sp_b):
    import jax
    import jax.numpy as jnp
    def _L0_conv_ref(x, proj_w, dw1_w3, dw1_b3, dw1_w5, dw1_b5, dw2_w7, dw2_b7, dw2_w9, dw2_b9, dw2_w11, dw2_b11, att1_w, att1_b, att2_w, att2_b, sp_w, sp_b):
        import jax, jax.numpy as jnp
        import numpy as np
        B, C, H, W = (16, 128, 160, 160)
        C2 = C // 2
        KS1 = [3, 5]
        KS2 = [7, 9, 11]
        DIL2 = 3

        def _dwconv(x, w, b, dilation):
            k = w.shape[-1]
            pad = dilation * (k // 2)
            y = jax.lax.conv_general_dilated(x, w, window_strides=(1, 1), padding=[(pad, pad), (pad, pad)], rhs_dilation=(dilation, dilation), dimension_numbers=('NCHW', 'OIHW', 'NCHW'), feature_group_count=x.shape[1])
            return y + b[None, :, None, None]

        def _route(x, att_w, att_b, conv_ws, conv_bs, dilation):
            pooled = x.mean(axis=(2, 3))
            logits = pooled @ att_w.T + att_b
            weights = jax.nn.softmax(logits, axis=1)
            idx = jnp.argmax(weights, axis=1)
            outs = jnp.stack([_dwconv(x, w, b, dilation) for w, b in zip(conv_ws, conv_bs)], axis=1)
            sel = jnp.take_along_axis(outs, idx[:, None, None, None, None], axis=1)[:, 0]
            return sel
        x_proj = jnp.einsum('bchw,oc->bohw', x, proj_w)
        att1 = _route(x_proj, att1_w, att1_b, [dw1_w3, dw1_w5], [dw1_b3, dw1_b5], 1)
        att2 = _route(att1, att2_w, att2_b, [dw2_w7, dw2_w9, dw2_w11], [dw2_b7, dw2_b9, dw2_b11], DIL2)
        out = jnp.concatenate([att1, att2], axis=1)
        avg_att = out.mean(axis=1, keepdims=True)
        max_att = out.max(axis=1, keepdims=True)
        att = jnp.concatenate([avg_att, max_att], axis=1)
        att = jax.lax.conv_general_dilated(att, sp_w, (1, 1), [(3, 3), (3, 3)], dimension_numbers=('NCHW', 'OIHW', 'NCHW'))
        att = jax.nn.sigmoid(att + sp_b[None, :, None, None])
        gate = att[:, 0:1] + att[:, 1:2]
        return out * gate + x

    def _gn(v, G=32, eps=1e-5):
        B_, C_, H_, W_ = v.shape
        g = v.reshape(B_, G, C_ // G, H_, W_)
        m = jnp.mean(g, axis=(2, 3, 4), keepdims=True)
        s = jnp.var(g, axis=(2, 3, 4), keepdims=True)
        return ((g - m) / jnp.sqrt(s + eps)).reshape(v.shape)

    def _ln_c(v, eps=1e-6):
        m = jnp.mean(v, axis=1, keepdims=True)
        s = jnp.var(v, axis=1, keepdims=True)
        return (v - m) / jnp.sqrt(s + eps)

    def _ln_t(v, eps=1e-5):
        m = jnp.mean(v, axis=-1, keepdims=True)
        s = jnp.var(v, axis=-1, keepdims=True)
        return (v - m) / jnp.sqrt(s + eps)

    def _to_tokens(v):
        B_, C_, H_, W_ = v.shape
        return v.reshape(B_, C_, H_ * W_).transpose(0, 2, 1)
    def _from_tokens(t, like):
        B_, C_, H_, W_ = like.shape
        return t.transpose(0, 2, 1).reshape(B_, C_, H_, W_)

    x = _L0_conv_ref(x, L0_conv_proj_w, L0_conv_dw1_w3, L0_conv_dw1_b3, L0_conv_dw1_w5, L0_conv_dw1_b5, L0_conv_dw2_w7, L0_conv_dw2_b7, L0_conv_dw2_w9, L0_conv_dw2_b9, L0_conv_dw2_w11, L0_conv_dw2_b11, L0_conv_att1_w, L0_conv_att1_b, L0_conv_att2_w, L0_conv_att2_b, L0_conv_sp_w, L0_conv_sp_b)
    return x


_drawn_inputs = setup_inputs


def setup_inputs(seed=0):
    import zlib

    import numpy as np

    out = dict(_drawn_inputs(seed))
    spreads = {'L0_conv_dw1_b3': (0.0, 0.1),
     'L0_conv_dw1_b5': (0.0, 0.1),
     'L0_conv_dw2_b7': (0.0, 0.1),
     'L0_conv_dw2_b9': (0.0, 0.1),
     'L0_conv_dw2_b11': (0.0, 0.1),
     'L0_conv_att1_b': (0.0, 0.1),
     'L0_conv_att2_b': (0.0, 0.1),
     'L0_conv_sp_b': (0.0, 0.8)}
    factors = {'L0_conv_sp_w': 8.0}
    for name, (base, spread) in spreads.items():
        noise = np.random.default_rng([zlib.crc32(name.encode()), seed]).standard_normal(out[name].shape)
        drawn = base * np.exp(spread * noise) if base else spread * noise
        out[name] = jnp.asarray(drawn.astype(out[name].dtype))
    for name, factor in factors.items():
        out[name] = (out[name] * factor).astype(out[name].dtype)
    return out
```

```python
from contextlib import ExitStack

import concourse.bass as bass
from concourse import mybir

ALU = mybir.AluOpType
ACT = mybir.ActivationFunctionType
AX = mybir.AxisListType
F32 = mybir.dt.float32
BF16 = mybir.dt.bfloat16
I32 = mybir.dt.int32

H = W = 160
PIX = H * W
C, C2 = 128, 64
K1 = (3, 5)
K2 = (7, 9, 11)
DIL = 3

Q1 = 4
RIN1, ROUT1 = 32, 28
NB1 = 6
T1 = W // Q1
TO1 = T1 + 1
N1 = NB1 * TO1
J1 = 11
WB1 = 8 * RIN1

NPH = DIL
RPH = 54
PO2 = 82
N2 = NPH * PO2
PADL = 3
PW = W + 2 * PADL
J2 = 13
WB2 = 12 * 64
SHIFTS2 = (0, -1, -2, -3, 1, 2)
RANGE2 = {0: (0, 82), -1: (2, 82), -2: (5, 82), -3: (8, 82), 1: (0, 77), 2: (0, 74)}

G = 4
NG = C2 // G
HROWS = NB1 * ROUT1
CHS = HROWS * W
CHUNK = 800
SUB = CHUNK // 2
FILLS = [(0, 7), (7, 14), (14, 20), (20, 27), (27, 34), (34, 40)]
NF = len(FILLS)
MAP_STEPS = 2 + 2 * C2
ROUTE_STEPS = 30
NEG = -3.4028235e38
SPB = 40


def conv_block(nc, x, proj_w, w1, b1, w2, b2, att1_w, att1_b, att2_w, att2_b, sp_w, sp_b, out):
    B = x.shape[0]
    ctx = ExitStack()
    with ctx:
        def sb(name, shape, dt=F32):
            return ctx.enter_context(nc.sbuf_tensor(name, shape, dt))

        def sem(name):
            return ctx.enter_context(nc.semaphore(name))

        def dram(name, shape, dt=F32):
            return nc.dram_tensor(name, shape, dt).ap()

        pad1_d = dram("pad1_d", (2 * C2 * J1, 64))
        pad2_d = dram("pad2_d", (3 * C2 * J2, 128))
        padsp_d = dram("padsp_d", (28, 128))
        band1_d = dram("band1_d", (RIN1, 2, C2, J1 * 32))
        band2_d = dram("band2_d", (64, 3, C2, J2 * 64))
        bandsp_d = dram("bandsp_d", (48, 28, 64))
        bias_d = dram("bias_d", (5, C2))
        att_d = dram("att_d", (B, C, CHS))
        map_d = dram("map_d", (B, 4, 168, W))
        gate_d = dram("gate_d", (B, 3, PIX), BF16)

        xs = sb("xs", [128, 2, RIN1, W])
        xr = sb("xr", [128, W, RIN1])
        xp = sb("xp", [128, C2, NB1, T1])
        w1t = sb("w1t", [128, 2, G, WB1])
        w2t = sb("w2t", [128, 2, 2, WB2])
        st1 = sb("st1", [128, 2, NB1 * W])
        st2 = sb("st2", [128, 2, 2, NPH * W])
        ph = sb("ph", [128, 2, G, NPH, PW])
        dx = sb("dx", [128, 2, CHUNK])
        da = sb("da", [128, 2, CHUNK])
        gmix = sb("gmix", [128, 1920], BF16)
        gt = gmix[0:3, 0:2 * CHUNK].rearrange("p (a n) -> p a n", a=2)
        gparts = gmix[64:64 + SPB, :].rearrange("p (a n) -> p a n", a=3)
        ones3 = sb("ones3", [3, 128], BF16)
        wsp = sb("wsp", [128, 7, 128])
        acc1 = sb("acc1", [128, 2, N1])
        acc2 = sb("acc2", [128, 2, N2])
        mina = sb("mina", [128, 4, W + 6])
        work = sb("work", [128, (NB1 + NPH) * W])
        nat1 = work[:, 0:NB1 * W]
        nat2 = work[:, NB1 * W:(NB1 + NPH) * W]
        minb = work[:, 0:4 * W].rearrange("p (b w) -> p b w", b=4)
        sg = work[64:64 + SPB, 0:2 * 640].rearrange("p (o n) -> p o n", o=2)
        wnat = sb("wnat", [C2, 285])
        spw = sb("spw", [1, 196])
        projt = sb("projt", [C, C2])
        a1t = sb("a1t", [C2, 2])
        a2t = sb("a2t", [C2, 3])
        b1n = sb("b1n", [C2, 2])
        attb = sb("attb", [1, 5])
        spbt = sb("spbt", [128, 2])
        bias1 = sb("bias1", [128, C2])
        bias2 = sb("bias2", [128, C2])
        part = sb("part", [128, NB1, 5])
        stats = sb("stats", [128, 5, 5])
        psx = sb("psx", [C2, 5, 5])
        srow = sb("srow", [C2, 5, 5])
        swin = sb("swin", [C2, 5, 5])
        wmul = sb("wmul", [C2, 25 + 9])
        pooled = sb("pooled", [C2, 3])
        lg = sb("lg", [1, 32])
        idx = sb("idx", [1, 2], I32)

        psP = [ctx.enter_context(nc.psum_tensor(f"psP{i}", [128, 512], F32)) for i in range(2)]
        ps1 = [ctx.enter_context(nc.psum_tensor(f"psConv1_{i}", [128, 512], F32)) for i in range(2)]
        ps2 = [ctx.enter_context(nc.psum_tensor(f"psConv2_{i}", [128, 512], F32)) for i in range(2)]
        psG = [ctx.enter_context(nc.psum_tensor(f"psGate{i}", [128, 512], F32)) for i in range(2)]

        xpf = xp[:, :, :, :].rearrange("p c b t -> p (c b t)")
        pad1 = xpf[0:C2, 0:2 * J1 * 64].rearrange("p (v j z) -> p v j z", v=2, j=J1)
        o2 = 2 * J1 * 64
        pad2 = xpf[0:C2, o2:o2 + 3 * J2 * 128].rearrange("p (v j z) -> p v j z", v=3, j=J2)
        o3 = o2 + 3 * J2 * 128
        padsp = xpf[0:1, o3:o3 + 28 * 128].rearrange("p (r z) -> p r z", z=128)
        oS = o3 + 28 * 128

        waits_met = sem("waits_met")
        s_wnat = sem("s_wnat")
        s_padzero = sem("s_padzero")
        s_pad = sem("s_pad")
        s_pad_d = sem("s_pad_d")
        s_band = sem("s_band")
        s_init = sem("s_init")
        s_wsp = sem("s_wsp")
        s_mapzero = sem("s_mapzero")
        x_loaded = [sem(f"x_loaded{i}") for i in range(2)]
        x_zeroed = sem("x_zeroed")
        stats_done = sem("stats_done")
        xr_ready = sem("xr_ready")
        proj_mm = sem("proj_mm")
        proj_evac = sem("proj_evac")
        stats_ready = sem("stats_ready")
        stats_mm = sem("stats_mm")
        route_steps = sem("route_steps")
        pool_ready = sem("pool_ready")
        logits_mm = sem("logits_mm")
        idx_ready = sem("idx_ready")
        bias_loaded = sem("bias_loaded")
        w1_loaded = [sem(f"w1_loaded{i}") for i in range(2)]
        w2_loaded = [sem(f"w2_loaded{i}") for i in range(2)]
        ph_loaded = [sem(f"ph_loaded{i}") for i in range(2)]
        conv1_mm = sem("conv1_mm")
        conv1_evac = sem("conv1_evac")
        acc1_steps = sem("acc1_steps")
        conv2_mm = sem("conv2_mm")
        conv2_evac = sem("conv2_evac")
        acc2_steps = sem("acc2_steps")
        att1_stored = [sem(f"att1_stored{i}") for i in range(2)]
        att2_stored = [sem(f"att2_stored{i}") for i in range(2)]
        nat_ready = sem("nat_ready")
        maps_stored = sem("maps_stored")
        min_loaded = sem("min_loaded")
        min_steps = sem("min_steps")
        sp_mm = sem("sp_mm")
        sig_done = sem("sig_done")
        gate_steps = sem("gate_steps")
        gate_stored = sem("gate_stored")
        d_loaded = [sem(f"d_loaded{i}") for i in range(2)]
        d_bc = sem("d_bc")
        d_mul = sem("d_mul")
        d_done = sem("d_done")
        out_stored = [sem(f"out_stored{i}") for i in range(2)]

        def wait(eng, s, value):
            if isinstance(value, int) and value <= 0:
                return
            eng.wait_ge(s, value)

        def wait_alone(eng, s, value):
            if isinstance(value, int) and value <= 0:
                return
            eng.wait_ge(s, value)
            eng.sem_inc(waits_met)

        def repeat(eng, lo, hi, body, written=0):
            for i in range(lo, min(lo + written, hi)):
                body(i)
            if lo + written < hi:
                with eng.Fori(lo + written, hi) as i:
                    body(i)

        def samples(eng, body):
            body(0, True, False)
            body(1, False, False)
            with eng.Fori(2, B - 1) as s:
                body(s, False, False)
            body(B - 1, False, True)

        def peel(s):
            return 1 if isinstance(s, int) and s < 2 else 0

        def neg_step(ap, count):
            return bass.AP(ap.tensor, ap.offset, [list(ap.ap[0]), [-1, count]])

        block = ctx.enter_context(nc.Block())

        @block.sync
        def _(sp):
            with nc.allow_non_contiguous_dma(reason="small weights, once"):
                o = 0
                for w in (*w1, *w2):
                    n = w.shape[2] * w.shape[3]
                    sp.dma_start(wnat[:, o:o + n], w.rearrange("c a h w -> c (a h w)")).then_inc(s_wnat, 16)
                    o += n
                sp.dma_start(spw[:, :], bass.AP(sp_w.tensor, sp_w.offset, [[196, 1], [1, 196]])).then_inc(s_wnat, 16)
                sp.dma_start(projt[:, :], proj_w.rearrange("o c -> c o")).then_inc(s_wnat, 16)
                sp.dma_start(a1t[:, :], att1_w.rearrange("o c -> c o")).then_inc(s_wnat, 16)
                sp.dma_start(a2t[:, :], att2_w.rearrange("o c -> c o")).then_inc(s_wnat, 16)
                for v in range(2):
                    sp.dma_start(b1n[:, v:v + 1], bass.AP(b1[v].tensor, 0, [[1, C2], [1, 1]])).then_inc(s_wnat, 16)
                sp.dma_start(attb[:, 0:2], bass.AP(att1_b.tensor, 0, [[2, 1], [1, 2]])).then_inc(s_wnat, 16)
                sp.dma_start(attb[:, 2:5], bass.AP(att2_b.tensor, 0, [[3, 1], [1, 3]])).then_inc(s_wnat, 16)
                sp.dma_start(spbt[:, :], bass.AP(sp_b.tensor, 0, [[0, 128], [1, 2]])).then_inc(s_wnat, 16)
                for v, b in enumerate((*b1, *b2)):
                    sp.dma_start(bias_d[v:v + 1, :], bass.AP(b.tensor, 0, [[C2, 1], [1, C2]])).then_inc(s_wnat, 16)

            def load_x(s, b):
                jb = s * NB1 + b
                wait(sp, xr_ready, 2 * (jb - 1))
                wait(sp, stats_done, jb - 1)
                lo, hi = max(0, ROUT1 * b - 2), min(H, ROUT1 * b + 30)
                i0 = lo - (ROUT1 * b - 2)
                sp.dma_start(xs[:, b % 2, i0:i0 + hi - lo, :], x[s, :, lo:hi, :]).then_inc(x_loaded[b % 2], 16)

            def load_w1(s, g, v1, q):
                wait(sp, conv1_mm, s * 32 + 2 * g - 2)
                for k in range(Q1):
                    src = band1_d[:, v1, bass.ds(g * G, G), (3 - k) * 32:(3 - k) * 32 + WB1]
                    sp.dma_start(w1t[32 * k:32 * k + 32, q, :, :], src).then_inc(w1_loaded[q], 16)

            def load_w2(s, g, v2, pr):
                wait(sp, conv2_mm, s * 32 + 2 * g + pr - 1)
                for k in range(2):
                    src = band2_d[:, v2, bass.ds(g * G + 2 * pr, 2), (1 - k) * 64:(1 - k) * 64 + WB2]
                    sp.dma_start(w2t[64 * k:64 * k + 64, pr, :, :], src).then_inc(w2_loaded[pr], 16)

            def load_phases(s, g, h, q):
                wait(sp, conv2_mm, s * 32 + 2 * g - 2)
                sp.wait_ge(att1_stored[q], 64 * (s * 8 + h + 1))
                for k in range(2):
                    o = PADL - DIL * k
                    for i0, n, r in ((0, 48, NPH), (48, 5, NPH), (53, 1, 1)):
                        for cc in range(G):
                            src = att_d[s, g * G + cc, :].rearrange("(i r w) -> i r w", r=NPH, w=W)
                            sp.dma_start(ph[64 * k + i0:64 * k + i0 + n, q, cc, 0:r, o:o + W],
                                         src[i0:i0 + n, 0:r, :]).then_inc(ph_loaded[q], 16)

            def load_chunk(sd, g, cp):
                n = sd * NG + g
                wait(sp, out_stored[cp], 16 * n)
                px = bass.ds((2 * g + cp) * CHUNK, CHUNK)
                xf = x[sd].rearrange("c h w -> c (h w)")
                sp.dma_start(dx[:, cp, :], xf[:, px]).then_inc(d_loaded[cp], 16)
                sp.dma_start(da[:, cp, :], att_d[sd, :, px]).then_inc(d_loaded[cp], 16)
                sp.dma_start(gt[:, cp, :], gate_d[sd, :, px]).then_inc(d_loaded[cp], 16)

            for b in range(2):
                load_x(0, b)
            sp.wait_ge(s_pad_d, 48)
            def expand(band, pad, rows, n, width):
                sp.dma_start(bass.AP(band.tensor, 0, [[width, n], [n * width, rows], [1, width]]),
                             bass.AP(pad.tensor, width - 1, [[2 * width, n], [-1, rows], [1, width]])).then_inc(s_band, 16)

            expand(band1_d, pad1_d, RIN1, 2 * C2 * J1, 32)
            expand(bandsp_d, padsp_d, 48, 28, 64)
            sp.wait_ge(s_band, 32)
            sp.wait_ge(s_init, 1)
            for i in range(2):
                sp.dma_start(wsp[64 * i:64 * i + 48, :, :].rearrange("p k (o z) -> p (k o) z", o=2),
                             bandsp_d[:, 14 * i:14 * i + 14, :]).then_inc(s_wsp, 16)
            expand(band2_d, pad2_d, 64, 3 * C2 * J2, 64)
            for b in range(2, NB1):
                load_x(0, b)
            sp.wait_ge(s_band, 48)

            def sample(s, first, last):
                wait_alone(sp, idx_ready, s + 1)
                v1 = sp.value_load(idx[0:1, 0:1], min_val=0, max_val=1)
                v2 = sp.value_load(idx[0:1, 1:2], min_val=0, max_val=2)
                wait_alone(sp, conv1_evac, 32 * s)
                wait_alone(sp, acc1_steps, MAP_STEPS * s)
                wait_alone(sp, conv2_evac, 32 * s)
                wait_alone(sp, acc2_steps, MAP_STEPS * s)
                if first:
                    sp.wait_ge(s_wnat, 16 * 19)
                sp.dma_start(bias1[:, :], bias_d[bass.ds(v1, 1), :].partition_broadcast(128)
                             if False else bass.AP(bias_d.tensor, v1 * C2, [[0, 128], [1, C2]])).then_inc(bias_loaded, 16)
                sp.dma_start(bias2[:, :], bass.AP(bias_d.tensor, v2 * C2 + 2 * C2, [[0, 128], [1, C2]])).then_inc(bias_loaded, 16)
                load_w1(s, 0, v1, 0)
                load_w1(s, 1, v1, 1)
                if not first:
                    for q in range(2):
                        wait_alone(sp, att1_stored[q], 512 * s)
                        wait_alone(sp, att2_stored[q], 512 * s)
                    wait_alone(sp, gate_stored, 48 * s)

                def groups(h):
                    for q in range(2):
                        load_w1(s, 2 * h + 2 + q, v1, q)
                        load_phases(s, 2 * h + q, h, q)
                        load_w2(s, 2 * h + q, v2, 0)
                        if not first:
                            load_chunk(s - 1, 2 * h + q, 0)
                        load_w2(s, 2 * h + q, v2, 1)
                        if not first:
                            load_chunk(s - 1, 2 * h + q, 1)

                repeat(sp, 0, 3, groups, peel(s))
                if not last:
                    load_x(s + 1, 0)
                repeat(sp, 3, 5, groups)
                if not last:
                    load_x(s + 1, 1)
                repeat(sp, 5, 7, groups)
                for q in range(2):
                    load_phases(s, 14 + q, 7, q)
                    load_w2(s, 14 + q, v2, 0)
                    if not first:
                        load_chunk(s - 1, 14 + q, 0)
                    if q == 0 and not last:
                        for b in range(2, NB1):
                            load_x(s + 1, b)
                    load_w2(s, 14 + q, v2, 1)
                    if not first:
                        load_chunk(s - 1, 14 + q, 1)

            samples(sp, sample)
            for q in range(2):
                sp.wait_ge(att1_stored[q], 512 * B)
                sp.wait_ge(att2_stored[q], 512 * B)
            sp.wait_ge(gate_stored, 48 * B)

            def last_chunks(g):
                for cp in range(2):
                    load_chunk(B - 1, g, cp)
            repeat(sp, 0, NG, last_chunks)

        @block.gpsimd
        def _(pool):
            nc.gpsimd.memset(xpf[0:C2, 0:oS], 0.0).then_inc(s_padzero, 1)
            nc.gpsimd.memset(xs[:, 0, 0:2, :], 0.0).then_inc(x_zeroed, 1)
            nc.gpsimd.memset(st1[0:4 * B, 0, :], 0.0)
            nc.gpsimd.memset(wsp[:, :, :], 0.0)
            nc.gpsimd.memset(mina[:, :, :], 0.0)
            nc.gpsimd.memset(ones3[:, :], 1.0)
            nc.gpsimd.memset(ph[:, :, :, :, :], 0.0).then_inc(s_init, 1)
            pool.wait_ge(s_init, 1)
            md = map_d.rearrange("b m h w -> (b m) (h w)")
            pool.dma_start(md[:, 0:3 * W], st1[0:4 * B, 0, 0:3 * W]).then_inc(s_mapzero, 16)
            pool.dma_start(md[:, 163 * W:168 * W], st1[0:4 * B, 0, 0:5 * W]).then_inc(s_mapzero, 16)

            def zero_rows(s, b):
                jb = s * NB1 + b
                wait_alone(pool, xr_ready, 2 * (jb - 1))
                wait_alone(pool, stats_done, jb - 1)
                rows = slice(0, 2) if b == 0 else slice(H - (ROUT1 * b - 2), RIN1)
                nc.gpsimd.memset(xs[:, b % 2, rows, :], 0.0).then_inc(x_zeroed, 1)

            def rearrange_x(s, b):
                jb = s * NB1 + b
                pool.wait_ge(x_loaded[b % 2], 16 * (3 * s + b // 2 + 1))
                if b == 0 or b == NB1 - 1:
                    pool.wait_ge(x_zeroed, 2 * s + (1 if b == 0 else 2))
                for hf in range(2):
                    wait_alone(pool, proj_mm, NF * (jb - 1) + 3 * hf + 3)
                    w = slice(hf * 80, hf * 80 + 80)
                    nc.gpsimd.tensor_copy(xr[:, w, :].rearrange("p w i -> p i w"), xs[:, b % 2, :, w]).then_inc(xr_ready, 1)

            for b in range(NB1):
                if b == NB1 - 1:
                    zero_rows(0, b)
                rearrange_x(0, b)

            def store_chunk(sd, g, cp):
                ci = (sd * NG + g) * 2 + cp
                pool.wait_ge(d_done, 2 * ci + 2)
                of = out[sd].rearrange("c h w -> c (h w)")
                pool.dma_start(of[:, bass.ds((2 * g + cp) * CHUNK, CHUNK)], dx[:, cp, :]).then_inc(out_stored[cp], 16)

            def sample(s, first, last):
                def groups(h):
                    for q in range(2):
                        for cp in range(2):
                            store_chunk(s - 1, 2 * h + q, cp)
                if not first:
                    repeat(pool, 0, 3, groups, peel(s))
                if not last:
                    zero_rows(s + 1, 0)
                if not first:
                    repeat(pool, 3, 7, groups)
                if not last:
                    for b in range(NB1):
                        if b == NB1 - 1:
                            zero_rows(s + 1, b)
                        rearrange_x(s + 1, b)
                if not first:
                    store_chunk(s - 1, 14, 0)
                    store_chunk(s - 1, 14, 1)
                    store_chunk(s - 1, 15, 0)
                    store_chunk(s - 1, 15, 1)
                pool.wait_ge(nat_ready, s + 1)
                if first:
                    pool.wait_ge(s_mapzero, 32)
                for m in range(2):
                    v = nat1[32 * m:32 * m + 28, :].rearrange("p (b w) -> p b w", w=W)
                    d = map_d[s, m, 3:3 + 140, :].rearrange("(b i) w -> i b w", i=ROUT1)
                    pool.dma_start(d, v[:, 0:5, :]).then_inc(maps_stored, 16)
                    pool.dma_start(map_d[s, m, 143:163, :], v[0:20, 5, :]).then_inc(maps_stored, 16)
                    v = nat2[64 * m:64 * m + RPH, :].rearrange("p (r w) -> p r w", w=W)
                    d = map_d[s, 2 + m, 3:3 + 159, :].rearrange("(i r) w -> i r w", r=NPH)
                    pool.dma_start(d[0:48, :, :], v[0:48, :, :]).then_inc(maps_stored, 16)
                    pool.dma_start(d[48:53, :, :], v[48:53, :, :]).then_inc(maps_stored, 16)
                    pool.dma_start(map_d[s, 2 + m, 162:163, :], v[53:54, 0, :]).then_inc(maps_stored, 16)
                pool.wait_ge(maps_stored, 160 * (s + 1))
                wait(pool, sp_mm, 2 * s)
                for m in range(2):
                    for k, t in enumerate((mina[:, :, 3:3 + W], minb)):
                        src = bass.AP(map_d.tensor, s * (4 * 168 * W) + (2 * k + m) * 168 * W,
                                      [[W, 48], [SPB * W, 4], [1, W]])
                        pool.dma_start(t[64 * m:64 * m + 48, :, :], src).then_inc(min_loaded, 16)
                pool.wait_ge(gate_steps, 6 * (s + 1))
                for k in range(3):
                    d = gate_d[s, k, :].rearrange("(b i w) -> i b w", i=SPB, w=W)
                    pool.dma_start(d, gparts[:, k, :].rearrange("p (b w) -> p b w", w=W)).then_inc(gate_stored, 16)

            samples(pool, sample)

            def last_chunks(g):
                for cp in range(2):
                    store_chunk(B - 1, g, cp)
            repeat(pool, 0, NG, last_chunks)
            for cp in range(2):
                pool.wait_ge(out_stored[cp], 16 * NG * B)
            pool.wait_ge(s_band, 48)
            pool.wait_ge(gate_stored, 48 * B)

        @block.scalar
        def _(act):
            act.wait_ge(s_pad, 3)
            act.dma_start(pad1_d.rearrange("(v c j) z -> c v (j z)", v=2, c=C2),
                          pad1.rearrange("p v j z -> p v (j z)")).then_inc(s_pad_d, 16)
            act.dma_start(padsp_d.rearrange("(a r) z -> a r z", a=1), padsp).then_inc(s_pad_d, 16)
            act.dma_start(pad2_d.rearrange("(v c j) z -> c v (j z)", v=3, c=C2),
                          pad2.rearrange("p v j z -> p v (j z)")).then_inc(s_pad_d, 16)
            act.wait_ge(s_pad_d, 48)

            def evac_proj(s, b2):
                for bb in range(2):
                    b = 2 * b2 + bb
                    for k, (t0, t1) in enumerate(FILLS):
                        n = (s * NB1 + b) * NF + k
                        act.wait_ge(proj_mm, n + 1)
                        dst = xp[:, :, b, t0:t1].rearrange("p c t -> p t c")
                        src = psP[k % 2][:, 0:64 * (t1 - t0)].rearrange("p (t c) -> p t c", c=C2)
                        nc.scalar.activation(dst, src, ACT.Identity).then_inc(proj_evac, 1)

            def evac_conv1(s, g, h, q):
                wait(act, att1_stored[q], 64 * (s * 8 + h))
                for pr in range(2):
                    P = s * 32 + 2 * g + pr
                    act.wait_ge(conv1_mm, P + 1)
                    for ch in range(2):
                        cc = 2 * pr + ch
                        ps = ps1[pr][:, ch * N1:(ch + 1) * N1].rearrange("p (b t) -> p b t", t=TO1)
                        dst = st1[32 * cc:32 * cc + ROUT1, q, :].rearrange("p (b t k) -> p b t k", b=NB1, k=Q1)
                        for k in range(Q1):
                            t0 = 1 if k < 2 else 0
                            ins = nc.scalar.activation(dst[:, :, :, (k + 2) % 4], ps[32 * k:32 * k + ROUT1, :, t0:t0 + T1],
                                                       ACT.Identity, bias=bias1[32 * k:32 * k + ROUT1, bass.ds(g * G + cc, 1)])
                    ins.then_inc(conv1_evac, 1)
                act.wait_ge(conv1_evac, s * 32 + 2 * g + 2)
                for cc in range(G):
                    d = att_d[s, g * G + cc, :].rearrange("(b i w) -> i b w", i=ROUT1, w=W)
                    act.dma_start(d, st1[32 * cc:32 * cc + ROUT1, q, :].rearrange("p (b w) -> p b w", w=W)
                                  ).then_inc(att1_stored[q], 16)

            def evac_conv2(s, g, h, q):
                wait(act, att2_stored[q], 64 * (s * 8 + h))
                for pr in range(2):
                    P = s * 32 + 2 * g + pr
                    act.wait_ge(conv2_mm, P + 1)
                    for ch in range(2):
                        ps = ps2[pr][:, ch * N2:(ch + 1) * N2].rearrange("p (r t) -> p r t", t=PO2)
                        dst = st2[64 * ch:64 * ch + RPH, q, pr, :].rearrange("p (r t k) -> p r t k", r=NPH, k=2)
                        for k in range(2):
                            p0 = 2 if k == 0 else 0
                            ins = nc.scalar.activation(dst[:, :, :, 1 - k], ps[64 * k:64 * k + RPH, :, p0:p0 + 80],
                                                       ACT.Identity, bias=bias2[64 * k:64 * k + RPH, bass.ds(g * G + 2 * pr + ch, 1)])
                    ins.then_inc(conv2_evac, 1)
                act.wait_ge(conv2_evac, s * 32 + 2 * g + 2)
                for ch in range(2):
                    for i0, n in ((0, 48), (48, 6)):
                        d = bass.AP(att_d.tensor, s * (C * CHS) + (g * G + C2 + ch) * CHS + i0 * NPH * W,
                                    [[NPH * W, n], [2 * CHS, 2], [1, NPH * W]])
                        act.dma_start(d, st2[64 * ch + i0:64 * ch + i0 + n, q, :, :]).then_inc(att2_stored[q], 16)

            repeat(act, 0, 3, lambda b2: evac_proj(0, b2))
            act.wait_ge(s_mapzero, 32)

            def sample(s, first, last):
                act.wait_ge(bias_loaded, 32 * (s + 1))
                evac_conv1(s, 0, 0, 0)
                evac_conv1(s, 1, 0, 1)

                def groups(h):
                    for q in range(2):
                        evac_conv1(s, 2 * h + 2 + q, h + 1, q)
                        evac_conv2(s, 2 * h + q, h, q)
                repeat(act, 0, 7, groups, peel(s))
                if not last:
                    act.wait_ge(conv1_mm, 32 * (s + 1))
                    repeat(act, 0, 3, lambda b2: evac_proj(s + 1, b2))
                for q in range(2):
                    evac_conv2(s, 14 + q, 7, q)
                for hf in range(2):
                    act.wait_ge(sp_mm, 2 * s + hf + 1)
                    if hf == 0:
                        wait(act, gate_steps, 6 * s)
                    for o in range(2):
                        ins = nc.scalar.activation(sg[:, o, 320 * hf:320 * hf + 320], psP[hf][64 * o:64 * o + SPB, 0:320],
                                                   ACT.Sigmoid, bias=spbt[64 * o:64 * o + SPB, o:o + 1])
                    ins.then_inc(sig_done, 1)

            samples(act, sample)
            for q in range(2):
                act.wait_ge(att1_stored[q], 512 * B)
                act.wait_ge(att2_stored[q], 512 * B)

        @block.tensor
        def _(pe):
            pe.wait_ge(s_wnat, 16 * 19)

            def project(s, b2):
                for bb in range(2):
                    b = 2 * b2 + bb
                    for k, (t0, t1) in enumerate(FILLS):
                        n = (s * NB1 + b) * NF + k
                        if k % 3 == 0:
                            pe.wait_ge(xr_ready, 2 * (s * NB1 + b) + k // 3 + 1)
                        wait(pe, proj_evac, n - 1)
                        for t in range(t0, t1):
                            lhsT = xr[:, Q1 * t:Q1 * t + Q1, :].rearrange("p q i -> p (q i)")
                            ins = nc.tensor.matmul(psP[k % 2][:, 64 * (t - t0):64 * (t - t0) + 64], lhsT, projt[:, :],
                                                   start=True, stop=True)
                        ins.then_inc(proj_mm, 1)

            def project_all(s):
                repeat(pe, 0, 3, lambda b2: project(s, b2), 1 if isinstance(s, int) and s == 0 else 0)

            def route(s):
                pe.wait_ge(stats_ready, s + 1)
                pe.wait_ge(proj_evac, NB1 * NF * (s + 1))
                nc.tensor.matmul(psP[0][0:C2, 0:25], projt[:, :], stats[:, :, :].rearrange("p r c -> p (r c)"),
                                 start=True, stop=True).then_inc(stats_mm, 1)
                wait_alone(pe, pool_ready, s + 1)
                for n, (o, m, rhs) in enumerate(((32, 2, a1t), (40, 3, a2t), (48, 3, a2t))):
                    ins = nc.tensor.matmul(psP[0][0:1, o:o + m], pooled[:, n:n + 1], rhs[:, :], start=True, stop=True)
                ins.then_inc(logits_mm, 1)

            def conv1(s, g, h, q):
                pe.wait_ge(w1_loaded[q], 64 * (s * 8 + h + 1))
                for pr in range(2):
                    wait(pe, acc1_steps, s * MAP_STEPS + 2 + 4 * (2 * g + pr - 1))
                    for ch in range(2):
                        cc = 2 * pr + ch
                        o = ps1[pr][:, ch * N1:(ch + 1) * N1].rearrange("p (b t) -> p b t", t=TO1)
                        rhs = xp[:, bass.ds(g * G + cc, 1), :, :].rearrange("p c b t -> p (c b) t")
                        nc.tensor.matmul(o[:, :, 0:T1], w1t[:, q, cc, 0:128], rhs, start=True, stop=False, skip_group_check=True)
                        ins = nc.tensor.matmul(o[:, :, 1:1 + T1], w1t[:, q, cc, 128:256], rhs, start=False, stop=True,
                                               skip_group_check=True)
                    ins.then_inc(conv1_mm, 1)

            def conv2(s, g, h, q, pr):
                if pr == 0:
                    pe.wait_ge(ph_loaded[q], 24 * 16 * (s * 8 + h + 1))
                pe.wait_ge(w2_loaded[pr], 32 * (s * NG + g + 1))
                wait(pe, acc2_steps, s * MAP_STEPS + 2 + 4 * (2 * g + pr - 1))
                for ch in range(2):
                    cc = 2 * pr + ch
                    o = ps2[pr][0:118, ch * N2:(ch + 1) * N2].rearrange("p (r t) -> p r t", t=PO2)
                    for d in SHIFTS2:
                        lo, hi = RANGE2[d]
                        f = PADL + 2 * lo + 6 * d
                        ins = nc.tensor.matmul(o[:, :, lo:hi], w2t[0:118, pr, ch, (4 - 2 * d) * 64:(4 - 2 * d) * 64 + 118],
                                               ph[0:118, q, cc, :, f:f + 2 * (hi - lo) - 1:2],
                                               start=(d == 0), stop=(d == SHIFTS2[-1]), skip_group_check=True)
                ins.then_inc(conv2_mm, 1)

            def broadcast(sd, g, cp):
                ci = (sd * NG + g) * 2 + cp
                pe.wait_ge(d_loaded[cp], 48 * (sd * NG + g + 1))
                wait(pe, d_done, 2 * ci)
                for sub in range(2):
                    nc.tensor.matmul(psG[sub][:, 0:SUB], ones3[:, :], gt[:, cp, sub * SUB:(sub + 1) * SUB],
                                     start=True, stop=True).then_inc(d_bc, 1)

            project_all(0)
            route(0)

            def sample(s, first, last):
                if first:
                    pe.wait_ge(s_init, 1)
                    pe.wait_ge(s_wsp, 32)
                conv1(s, 0, 0, 0)
                conv1(s, 1, 0, 1)

                def groups(h):
                    for q in range(2):
                        g = 2 * h + q
                        conv1(s, g + 2, h + 1, q)
                        if not first:
                            broadcast(s - 1, g, 0)
                        conv2(s, g, h, q, 0)
                        if not first:
                            broadcast(s - 1, g, 1)
                        conv2(s, g, h, q, 1)
                repeat(pe, 0, 7, groups, peel(s))
                if not last:
                    wait_alone(pe, sig_done, 2 * s)
                    project_all(s + 1)
                for q in range(2):
                    g = 14 + q
                    if not first:
                        broadcast(s - 1, g, 0)
                    conv2(s, g, 7, q, 0)
                    if not first:
                        broadcast(s - 1, g, 1)
                    conv2(s, g, 7, q, 1)
                if not last:
                    route(s + 1)
                    pe.wait_ge(idx_ready, s + 2)
                else:
                    wait(pe, sig_done, 2 * s)
                pe.wait_ge(min_steps, 3 * (s + 1))
                for hf in range(2):
                    for kw in range(7):
                        ins = nc.tensor.matmul(psP[hf][0:104, 0:320], wsp[0:112, kw, 0:104], mina[0:112, 2 * hf:2 * hf + 2, kw:kw + W],
                                               start=(kw == 0), stop=(kw == 6))
                    ins.then_inc(sp_mm, 1)

            samples(pe, sample)

            def last_chunks(g):
                for cp in range(2):
                    broadcast(B - 1, g, cp)
            repeat(pe, 0, NG, last_chunks)

        @block.vector
        def _(dve):
            dve.wait_ge(s_padzero, 1)
            dve.wait_ge(s_wnat, 16 * 19)
            o = 0
            for dst, ks, kmax, z0, jn in ((pad1, K1, 5, 31, 7), (pad2, K2, 11, 68, 11)):
                for v, k in enumerate(ks):
                    e = (kmax - k) // 2
                    for kh in range(k):
                        src = wnat[:, o + kh * k + k - 1:o + kh * k + k]
                        ins = nc.vector.tensor_copy(dst[:, v, jn - e - (k - 1):jn - e + 1, z0 - e - kh], neg_step(src, k))
                    o += k * k
                ins.then_inc(s_pad, 1)
            for kh in range(7):
                for i in range(2):
                    ins = nc.vector.tensor_copy(
                        padsp[:, 14 * i:14 * i + 14, 63 - kh].rearrange("p (k o) -> p o k", o=2),
                        spw[:, :].rearrange("p (o i h w) -> p o i h w", o=2, i=2, h=7)[:, :, i, kh, :])
            ins.then_inc(s_pad, 1)

            def stats_block(s, b):
                q = b % 2
                dve.wait_ge(x_loaded[q], 16 * (3 * s + b // 2 + 1))
                own = slice(2, 2 + (ROUT1 if b < NB1 - 1 else H - ROUT1 * (NB1 - 1)))
                if b == 0 or b == NB1 - 1:
                    r0, i0 = (1, 2) if b == 0 else (3, 20)
                    nc.vector.tensor_reduce(stats[:, r0:r0 + 2, 0], xs[:, q, i0:i0 + 2, :], AX.X, ALU.add)
                    nc.vector.tensor_copy(stats[:, r0:r0 + 2, 1:3], xs[:, q, i0:i0 + 2, 0:2])
                    nc.vector.tensor_copy(stats[:, r0:r0 + 2, 3:5], xs[:, q, i0:i0 + 2, W - 2:W])
                nc.vector.tensor_reduce(part[:, b, 1:3], xs[:, q, own, 0:2].rearrange("p i w -> p w i"), AX.X, ALU.add)
                nc.vector.tensor_reduce(part[:, b, 3:5], xs[:, q, own, W - 2:W].rearrange("p i w -> p w i"), AX.X, ALU.add)
                nc.vector.tensor_reduce(part[:, b, 0:1], xs[:, q, own, :], AX.XY, ALU.add).then_inc(stats_done, 1)

            def stats_total(s):
                dve.wait_ge(stats_done, NB1 * (s + 1))
                nc.vector.tensor_reduce(stats[:, 0, :], part[:, :, :].rearrange("p b k -> p k b"), AX.X,
                                        ALU.add).then_inc(stats_ready, 1)

            def route(s):
                n = [0]

                def step(ins):
                    n[0] += 1
                    ins.then_inc(route_steps, 1)
                    dve.wait_ge(route_steps, s * ROUTE_STEPS + n[0])

                dve.wait_ge(stats_mm, s + 1)
                step(nc.vector.tensor_copy(psx[:, :, :].rearrange("p r c -> p (r c)"), psP[0][0:C2, 0:25]))
                for dst, src, ax in ((srow, psx, 0), (swin, srow, 1)):
                    def line(t, k):
                        return t[:, k, :] if ax == 0 else t[:, :, k]
                    step(nc.vector.tensor_copy(line(dst, 2), line(src, 0)))
                    step(nc.vector.tensor_tensor(line(dst, 1), line(src, 0), line(src, 4), ALU.subtract))
                    step(nc.vector.tensor_tensor(line(dst, 0), line(dst, 1), line(src, 3), ALU.subtract))
                    step(nc.vector.tensor_tensor(line(dst, 3), line(src, 0), line(src, 1), ALU.subtract))
                    step(nc.vector.tensor_tensor(line(dst, 4), line(dst, 3), line(src, 2), ALU.subtract))
                step(nc.vector.tensor_tensor(wmul[:, 0:9].rearrange("p (a b) -> p a b", a=3),
                                             wnat[:, 0:9].rearrange("p (a b) -> p a b", a=3), swin[:, 1:4, 1:4], ALU.mult))
                step(nc.vector.tensor_tensor(wmul[:, 9:34], wnat[:, 9:34], swin[:, :, :].rearrange("p a b -> p (a b)"), ALU.mult))
                step(nc.vector.tensor_reduce(pooled[:, 1:2], wmul[:, 0:9], AX.X, ALU.add))
                step(nc.vector.tensor_reduce(pooled[:, 2:3], wmul[:, 9:34], AX.X, ALU.add))
                step(nc.vector.tensor_scalar(pooled[:, 1:3], pooled[:, 1:3], 1.0 / PIX, None, ALU.mult))
                step(nc.vector.tensor_tensor(pooled[:, 1:3], pooled[:, 1:3], b1n[:, :], ALU.add))
                nc.vector.tensor_scalar(pooled[:, 0:1], psx[:, 0, 0:1], 1.0 / PIX, None, ALU.mult).then_inc(pool_ready, 1)
                dve.wait_ge(logits_mm, s + 1)
                step(nc.vector.tensor_tensor(lg[:, 0:2], psP[0][0:1, 32:34], attb[:, 0:2], ALU.add))
                step(nc.vector.tensor_tensor(lg[:, 2:5], psP[0][0:1, 40:43], attb[:, 2:5], ALU.add))
                step(nc.vector.tensor_tensor(lg[:, 5:8], psP[0][0:1, 48:51], attb[:, 2:5], ALU.add))
                l2 = lg[:, 2:8].rearrange("p (v k) -> p v k", k=3)
                step(nc.vector.tensor_tensor(lg[:, 8:9], lg[:, 1:2], lg[:, 0:1], ALU.is_gt))
                step(nc.vector.tensor_tensor(lg[:, 10:12], l2[:, :, 1], l2[:, :, 0], ALU.is_gt))
                step(nc.vector.tensor_tensor(lg[:, 12:14], l2[:, :, 1], l2[:, :, 0], ALU.max))
                step(nc.vector.tensor_tensor(lg[:, 14:16], l2[:, :, 2], lg[:, 12:14], ALU.is_gt))
                step(nc.vector.tensor_scalar(lg[:, 16:18], lg[:, 10:12], -1.0, 2.0, ALU.mult, ALU.add))
                step(nc.vector.tensor_tensor(lg[:, 18:20], lg[:, 16:18], lg[:, 14:16], ALU.mult))
                step(nc.vector.tensor_tensor(lg[:, 20:22], lg[:, 18:20], lg[:, 10:12], ALU.add))
                step(nc.vector.tensor_tensor(lg[:, 22:23], lg[:, 21:22], lg[:, 20:21], ALU.subtract))
                step(nc.vector.tensor_tensor(lg[:, 23:24], lg[:, 22:23], lg[:, 8:9], ALU.mult))
                step(nc.vector.tensor_tensor(lg[:, 9:10], lg[:, 23:24], lg[:, 20:21], ALU.add))
                wait(dve, bias_loaded, 32 * s)
                nc.vector.tensor_copy(idx[:, :], lg[:, 8:10]).then_inc(idx_ready, 1)
                assert n[0] == ROUTE_STEPS

            def init_maps(s):
                if not (isinstance(s, int) and s == 0):
                    dve.wait_ge(nat_ready, s)
                for a, steps in ((acc1, acc1_steps), (acc2, acc2_steps)):
                    nc.vector.memset(a[:, 0, :], 0.0).then_inc(steps, 1)
                    nc.vector.memset(a[:, 1, :], NEG).then_inc(steps, 1)

            def update_maps(s, g, pr, which):
                a, bias, ps, n, lanes, steps, evac = (
                    (acc1, bias1, ps1, N1, 128, acc1_steps, conv1_evac) if which == 1 else
                    (acc2, bias2, ps2, N2, 118, acc2_steps, conv2_evac))
                dve.wait_ge(evac, s * 32 + 2 * g + pr + 1)
                for ch in range(2):
                    src = ps[pr][0:lanes, ch * n:(ch + 1) * n]
                    bb = bias[0:lanes, bass.ds(g * G + 2 * pr + ch, 1)]
                    for m, op in ((0, ALU.add), (1, ALU.max)):
                        k = 2 + 2 * ch + m
                        dve.wait_ge(steps, s * MAP_STEPS + 4 * (2 * g + pr) + k - 1)
                        nc.vector.scalar_tensor_tensor(out=a[0:lanes, m, :], in0=src, scalar=bb, in1=a[0:lanes, m, :],
                                                       op0=ALU.add, op1=op).then_inc(steps, 1)

            def gate_chunk(sd, g, cp):
                ci = (sd * NG + g) * 2 + cp
                dve.wait_ge(d_loaded[cp], 48 * (sd * NG + g + 1))
                for sub in range(2):
                    px = slice(sub * SUB, (sub + 1) * SUB)
                    dve.wait_ge(d_bc, 2 * ci + sub + 1)
                    nc.vector.tensor_tensor(psG[sub][:, 0:SUB], psG[sub][:, 0:SUB], da[:, cp, px], ALU.mult).then_inc(d_mul, 1)
                for sub in range(2):
                    px = slice(sub * SUB, (sub + 1) * SUB)
                    dve.wait_ge(d_mul, 2 * ci + sub + 1)
                    nc.vector.tensor_tensor(dx[:, cp, px], psG[sub][:, 0:SUB], dx[:, cp, px], ALU.add).then_inc(d_done, 1)

            def copy_out_maps(s):
                dve.wait_ge(acc1_steps, MAP_STEPS * (s + 1))
                dve.wait_ge(acc2_steps, MAP_STEPS * (s + 1))
                wait(dve, maps_stored, 160 * s)
                for m in range(2):
                    a = acc1[:, m, :].rearrange("p (b t) -> p b t", t=TO1)
                    d = nat1[32 * m:32 * m + ROUT1, :].rearrange("p (b t k) -> p b t k", b=NB1, k=Q1)
                    for k in range(Q1):
                        t0 = 1 if k < 2 else 0
                        nc.vector.tensor_copy(d[:, :, :, (k + 2) % 4], a[32 * k:32 * k + ROUT1, :, t0:t0 + T1])
                    a = acc2[:, m, :].rearrange("p (r t) -> p r t", t=PO2)
                    d = nat2[64 * m:64 * m + RPH, :].rearrange("p (r t k) -> p r t k", r=NPH, k=2)
                    for k in range(2):
                        p0 = 2 if k == 0 else 0
                        ins = nc.vector.tensor_copy(d[:, :, :, 1 - k], a[64 * k:64 * k + RPH, :, p0:p0 + 80])
                ins.then_inc(nat_ready, 1)

            def combine_maps(s):
                dve.wait_ge(min_loaded, 64 * (s + 1))
                px = slice(3, 3 + W)
                nc.vector.tensor_tensor(mina[64:112, :, px], mina[64:112, :, px], minb[64:112, :, :], ALU.max).then_inc(min_steps, 1)
                nc.vector.tensor_tensor(mina[0:48, :, px], mina[0:48, :, px], minb[0:48, :, :], ALU.add).then_inc(min_steps, 1)
                dve.wait_ge(min_steps, 3 * s + 2)
                nc.vector.tensor_scalar(mina[0:48, :, px], mina[0:48, :, px], 1.0 / C, None, ALU.mult).then_inc(min_steps, 1)

            def gate(s):
                dve.wait_ge(sig_done, 2 * (s + 1))
                wait(dve, gate_stored, 48 * s)
                nc.vector.tensor_tensor(sg[:, 0, :], sg[:, 0, :], sg[:, 1, :], ALU.add).then_inc(gate_steps, 1)
                for k in range(3):
                    dve.wait_ge(gate_steps, 6 * s + 2 * k + 1)
                    nc.vector.tensor_copy(gparts[:, k, :], sg[:, k % 2, :]).then_inc(gate_steps, 1)
                    if k < 2:
                        dve.wait_ge(gate_steps, 6 * s + 2 * k + 2)
                        nc.vector.tensor_tensor(sg[:, 1 - k % 2, :], sg[:, k % 2, :], gparts[:, k, :],
                                                ALU.subtract).then_inc(gate_steps, 1)

            for b in range(NB1):
                stats_block(0, b)
            stats_total(0)
            route(0)

            def sample(s, first, last):
                init_maps(s)
                dve.wait_ge(bias_loaded, 32 * (s + 1))
                for g in range(2):
                    for pr in range(2):
                        update_maps(s, g, pr, 1)

                def groups(h):
                    for q in range(2):
                        g = 2 * h + q
                        for pr in range(2):
                            update_maps(s, g + 2, pr, 1)
                        for pr in range(2):
                            if not first:
                                gate_chunk(s - 1, g, pr)
                            update_maps(s, g, pr, 2)
                repeat(dve, 0, 3, groups, peel(s))
                if not last:
                    stats_block(s + 1, 0)
                repeat(dve, 3, 5, groups)
                if not last:
                    stats_block(s + 1, 1)
                repeat(dve, 5, 7, groups)
                if not last:
                    for b in range(2, NB1):
                        stats_block(s + 1, b)
                for g in (14, 15):
                    for pr in range(2):
                        if not first:
                            gate_chunk(s - 1, g, pr)
                        update_maps(s, g, pr, 2)
                if not last:
                    stats_total(s + 1)
                copy_out_maps(s)
                if not last:
                    route(s + 1)
                combine_maps(s)
                gate(s)

            samples(dve, sample)

            def last_chunks(g):
                for cp in range(2):
                    gate_chunk(B - 1, g, cp)
            repeat(dve, 0, NG, last_chunks)


_INS = ['x', 'L0_conv_proj_w', 'L0_conv_dw1_w3', 'L0_conv_dw1_b3', 'L0_conv_dw1_w5', 'L0_conv_dw1_b5',
        'L0_conv_dw2_w7', 'L0_conv_dw2_b7', 'L0_conv_dw2_w9', 'L0_conv_dw2_b9', 'L0_conv_dw2_w11', 'L0_conv_dw2_b11',
        'L0_conv_att1_w', 'L0_conv_att1_b', 'L0_conv_att2_w', 'L0_conv_att2_b', 'L0_conv_sp_w', 'L0_conv_sp_b']


def kernel(**inputs):
    import numpy as _np
    import concourse.bacc as _bacc
    from concourse import mybir as _mybir
    from concourse.bass_utils import run_bass_kernel_spmd as _run

    nc = _bacc.Bacc("TRN2", target_bir_lowering=False, num_devices=1)
    arrays, a = {}, {}
    for name in _INS:
        v = _np.ascontiguousarray(inputs[name])
        arrays[f"in_{name}_dram"] = v
        a[name.replace("L0_conv_", "")] = nc.dram_tensor(f"in_{name}_dram", v.shape, _mybir.dt.from_np(v.dtype),
                                                         kind="ExternalInput").ap()
    x = a["x"]
    out = nc.dram_tensor("out_0_dram", tuple(inputs["x"].shape), F32, kind="ExternalOutput").ap()
    conv_block(nc, x, a["proj_w"], [a["dw1_w3"], a["dw1_w5"]], [a["dw1_b3"], a["dw1_b5"]],
               [a["dw2_w7"], a["dw2_w9"], a["dw2_w11"]], [a["dw2_b7"], a["dw2_b9"], a["dw2_b11"]],
               a["att1_w"], a["att1_b"], a["att2_w"], a["att2_b"], a["sp_w"], a["sp_b"], out)
    r = _run(nc, [arrays], core_ids=[0])
    return r.results[0]["out_0_dram"]
```

```python
from contextlib import ExitStack

import concourse.bass as bass
from concourse import mybir

ALU = mybir.AluOpType
ACT = mybir.ActivationFunctionType
AX = mybir.AxisListType
F32 = mybir.dt.float32
BF16 = mybir.dt.bfloat16
I32 = mybir.dt.int32

H = W = 160
PIX = H * W
C, C2 = 128, 64
K1 = (3, 5)
K2 = (7, 9, 11)
DIL = 3

Q1 = 4
RIN1, ROUT1 = 32, 28
NB1 = 6
T1 = W // Q1
TO1 = T1 + 1
N1 = NB1 * TO1
J1 = 11
WB1 = 8 * RIN1

NPH = DIL
RPH = 54
PO2 = 82
N2 = NPH * PO2
PADL = 3
PW = W + 2 * PADL
J2 = 13
WB2 = J2 * 64
SHIFTS2 = (0, -1, -2, -3, 1, 2)
RANGE2 = {0: (0, 82), -1: (2, 82), -2: (5, 82), -3: (8, 82), 1: (0, 77), 2: (0, 74)}

G = 4
NG = C2 // G
HROWS = NB1 * ROUT1
CHS = HROWS * W
CHUNK = 800
SUB = CHUNK // 2
FILLS = [(0, 7), (7, 14), (14, 20), (20, 27), (27, 34), (34, 40)]
NF = len(FILLS)
MAP_STEPS = 2 + 2 * C2
MEAN_STEPS, ROUTE_STEPS = 17, 30
NEG = -3.4028235e38
SPB = 40


def conv_block(nc, x, proj_w, w1, b1, w2, b2, att1_w, att1_b, att2_w, att2_b, sp_w, sp_b, out):
    B = x.shape[0]
    ctx = ExitStack()
    with ctx:
        def sb(name, shape, dt=F32):
            return ctx.enter_context(nc.sbuf_tensor(name, shape, dt))

        def sem(name):
            return ctx.enter_context(nc.semaphore(name))

        def dram(name, shape, dt=F32):
            return nc.dram_tensor(name, shape, dt).ap()

        pad1_d = dram("pad1_d", (2 * C2 * J1, 64))
        pad2_d = dram("pad2_d", (3 * C2 * J2, 128))
        padsp_d = dram("padsp_d", (28, 128))
        band1_d = dram("band1_d", (RIN1, 2, C2, J1 * 32))
        band2_d = dram("band2_d", (64, 3, C2, J2 * 64))
        bandsp_d = dram("bandsp_d", (48, 28, 64))
        bias_d = dram("bias_d", (5, C2))
        att_d = dram("att_d", (B, C, CHS))
        map_d = dram("map_d", (B, 4, 168, W))
        gate_d = dram("gate_d", (B, 3, PIX), BF16)

        xs = sb("xs", [128, 2, RIN1, W])
        xr = sb("xr", [128, W, RIN1])
        xp = sb("xp", [128, C2, NB1, T1])
        w1t = sb("w1t", [128, 2, G, WB1])
        w2t = sb("w2t", [128, G, WB2])
        st1 = sb("st1", [128, 2, NB1 * W])
        st2 = sb("st2", [128, 2, 2, NPH * W])
        ph = sb("ph", [128, 2, G, NPH, PW])
        dx = sb("dx", [128, 2, CHUNK])
        da = sb("da", [128, 2, CHUNK])
        gmix = sb("gmix", [128, 1920], BF16)
        gt = gmix[0:3, 0:2 * CHUNK].rearrange("p (a n) -> p a n", a=2)
        gparts = gmix[64:64 + SPB, :].rearrange("p (a n) -> p a n", a=3)
        ones3 = sb("ones3", [3, 128], BF16)
        wsp = sb("wsp", [128, 7, 128])
        acc1 = sb("acc1", [128, 2, N1])
        acc2 = sb("acc2", [128, 2, N2])
        mina = sb("mina", [128, 4, W + 6])
        work = sb("work", [128, (NB1 + NPH) * W])
        nat1 = work[:, 0:NB1 * W]
        nat2 = work[:, NB1 * W:(NB1 + NPH) * W]
        minb = work[:, 0:4 * W].rearrange("p (b w) -> p b w", b=4)
        sg = work[64:64 + SPB, 0:2 * 640].rearrange("p (o n) -> p o n", o=2)
        wnat = sb("wnat", [C2, 285])
        spw = sb("spw", [1, 196])
        projt = sb("projt", [C, C2])
        a1t = sb("a1t", [C2, 2])
        a2t = sb("a2t", [C2, 3])
        b1n = sb("b1n", [C2, 2])
        attb = sb("attb", [1, 5])
        spbt = sb("spbt", [128, 2])
        bias1 = sb("bias1", [128, C2])
        bias2 = sb("bias2", [128, C2])
        part = sb("part", [128, NB1, 6])
        stats = sb("stats", [128, 5, 5])
        psx = sb("psx", [C2, 5, 5])
        srow = sb("srow", [C2, 5, 5])
        swin = sb("swin", [C2, 5, 5])
        wmul = sb("wmul", [C2, 25 + 9])
        pooled = sb("pooled", [C2, 3])
        lg = sb("lg", [1, 32])
        idx = sb("idx", [1, 2], I32)

        psP = [ctx.enter_context(nc.psum_tensor(f"psP{i}", [128, 512], F32)) for i in range(2)]
        ps1 = [ctx.enter_context(nc.psum_tensor(f"psConv1_{i}", [128, 512], F32)) for i in range(2)]
        ps2 = [ctx.enter_context(nc.psum_tensor(f"psConv2_{i}", [128, 512], F32)) for i in range(2)]
        psG = [ctx.enter_context(nc.psum_tensor(f"psGate{i}", [128, 512], F32)) for i in range(2)]

        xpf = xp[:, :, :, :].rearrange("p c b t -> p (c b t)")
        pad1 = xpf[0:C2, 0:2 * J1 * 64].rearrange("p (v j z) -> p v j z", v=2, j=J1)
        o2 = 2 * J1 * 64
        pad2 = xpf[0:C2, o2:o2 + 3 * J2 * 128].rearrange("p (v j z) -> p v j z", v=3, j=J2)
        o3 = o2 + 3 * J2 * 128
        padsp = xpf[0:1, o3:o3 + 28 * 128].rearrange("p (r z) -> p r z", z=128)
        oS = o3 + 28 * 128

        waits_met = sem("waits_met")
        s_wnat = sem("s_wnat")
        s_padzero = sem("s_padzero")
        s_pad = sem("s_pad")
        s_pad_d = sem("s_pad_d")
        s_band = sem("s_band")
        s_init = sem("s_init")
        s_wsp = sem("s_wsp")
        s_mapzero = sem("s_mapzero")
        x_loaded = [sem(f"x_loaded{i}") for i in range(2)]
        x_zeroed = sem("x_zeroed")
        xr_ready = sem("xr_ready")
        proj_mm = sem("proj_mm")
        proj_evac = sem("proj_evac")
        stats_ready = sem("stats_ready")
        stats_mm = sem("stats_mm")
        route_steps = sem("route_steps")
        pool_ready = sem("pool_ready")
        logits_mm = sem("logits_mm")
        idx_ready = sem("idx_ready")
        bias_loaded = sem("bias_loaded")
        w1_loaded = [sem(f"w1_loaded{i}") for i in range(2)]
        w2_loaded = [sem(f"w2_loaded{i}") for i in range(G)]
        w2_copied = sem("w2_copied")
        ph_loaded = [sem(f"ph_loaded{i}") for i in range(2)]
        ph_copied = sem("ph_copied")
        conv1_mm = sem("conv1_mm")
        conv1_evac = sem("conv1_evac")
        acc1_steps = sem("acc1_steps")
        conv2_mm = sem("conv2_mm")
        conv2_evac = sem("conv2_evac")
        acc2_steps = sem("acc2_steps")
        att1_stored = [sem(f"att1_stored{i}") for i in range(2)]
        att2_stored = [sem(f"att2_stored{i}") for i in range(2)]
        nat_ready = sem("nat_ready")
        maps_stored = [sem(f"maps_stored{m}") for m in range(2)]
        min_loaded = sem("min_loaded")
        min_steps = sem("min_steps")
        sp_mm = sem("sp_mm")
        sig_done = sem("sig_done")
        gate_steps = sem("gate_steps")
        gate_stored = sem("gate_stored")
        d_loaded = [sem(f"d_loaded{i}") for i in range(2)]
        d_bc = sem("d_bc")
        d_mul = sem("d_mul")
        d_done = sem("d_done")
        out_stored = [sem(f"out_stored{i}") for i in range(2)]

        def wait(eng, s, value):
            if isinstance(value, int) and value <= 0:
                return
            eng.wait_ge(s, value)

        def wait_alone(eng, s, value):
            if isinstance(value, int) and value <= 0:
                return
            eng.wait_ge(s, value)
            eng.sem_inc(waits_met)

        def repeat(eng, lo, hi, body, written=0):
            for i in range(lo, min(lo + written, hi)):
                body(i)
            if lo + written < hi:
                with eng.Fori(lo + written, hi) as i:
                    body(i)

        def samples(eng, body):
            body(0, True, False)
            body(1, False, False)
            with eng.Fori(2, B - 1) as s:
                body(s, False, False)
            body(B - 1, False, True)

        def peel(s):
            return 1 if isinstance(s, int) and s < 2 else 0

        def neg_step(ap, count):
            return bass.AP(ap.tensor, ap.offset, [list(ap.ap[0]), [-1, count]])

        def store_maps(eng, s, m):
            wait_alone(eng, nat_ready, s + 1)
            v = nat1[32 * m:32 * m + 28, :].rearrange("p (b w) -> p b w", w=W)
            d = map_d[s, m, 3:3 + 140, :].rearrange("(b i) w -> i b w", i=ROUT1)
            eng.dma_start(d, v[:, 0:5, :]).then_inc(maps_stored[m], 16)
            eng.dma_start(map_d[s, m, 143:163, :], v[0:20, 5, :]).then_inc(maps_stored[m], 16)
            v = nat2[64 * m:64 * m + RPH, :].rearrange("p (r w) -> p r w", w=W)
            d = map_d[s, 2 + m, 3:3 + 159, :].rearrange("(i r) w -> i r w", r=NPH)
            eng.dma_start(d[0:48, :, :], v[0:48, :, :]).then_inc(maps_stored[m], 16)
            eng.dma_start(d[48:53, :, :], v[48:53, :, :]).then_inc(maps_stored[m], 16)
            eng.dma_start(map_d[s, 2 + m, 162:163, :], v[53:54, 0, :]).then_inc(maps_stored[m], 16)

        block = ctx.enter_context(nc.Block())

        @block.sync
        def _(sp):
            with nc.allow_non_contiguous_dma(reason="small weights, once"):
                o = 0
                for w in (*w1, *w2):
                    n = w.shape[2] * w.shape[3]
                    sp.dma_start(wnat[:, o:o + n], w.rearrange("c a h w -> c (a h w)")).then_inc(s_wnat, 16)
                    o += n
                sp.dma_start(spw[:, :], bass.AP(sp_w.tensor, sp_w.offset, [[196, 1], [1, 196]])).then_inc(s_wnat, 16)
                sp.dma_start(projt[:, :], proj_w.rearrange("o c -> c o")).then_inc(s_wnat, 16)
                sp.dma_start(a1t[:, :], att1_w.rearrange("o c -> c o")).then_inc(s_wnat, 16)
                sp.dma_start(a2t[:, :], att2_w.rearrange("o c -> c o")).then_inc(s_wnat, 16)
                for v in range(2):
                    sp.dma_start(b1n[:, v:v + 1], bass.AP(b1[v].tensor, 0, [[1, C2], [1, 1]])).then_inc(s_wnat, 16)
                sp.dma_start(attb[:, 0:2], bass.AP(att1_b.tensor, 0, [[2, 1], [1, 2]])).then_inc(s_wnat, 16)
                sp.dma_start(attb[:, 2:5], bass.AP(att2_b.tensor, 0, [[3, 1], [1, 3]])).then_inc(s_wnat, 16)
                sp.dma_start(spbt[:, :], bass.AP(sp_b.tensor, 0, [[0, 128], [1, 2]])).then_inc(s_wnat, 16)
                for v, b in enumerate((*b1, *b2)):
                    sp.dma_start(bias_d[v:v + 1, :], bass.AP(b.tensor, 0, [[C2, 1], [1, C2]])).then_inc(s_wnat, 16)

            def load_x(s, b):
                jb = s * NB1 + b
                wait(sp, xr_ready, 2 * (jb - 1))
                lo, hi = max(0, ROUT1 * b - 2), min(H, ROUT1 * b + 30)
                i0 = lo - (ROUT1 * b - 2)
                sp.dma_start(xs[:, b % 2, i0:i0 + hi - lo, :], x[s, :, lo:hi, :]).then_inc(x_loaded[b % 2], 16)

            def load_w1(s, g, v1, q):
                wait(sp, conv1_mm, s * 32 + 2 * g - 2)
                for k in range(Q1):
                    src = band1_d[:, v1, bass.ds(g * G, G), (3 - k) * 32:(3 - k) * 32 + WB1]
                    sp.dma_start(w1t[32 * k:32 * k + 32, q, :, :], src).then_inc(w1_loaded[q], 16)

            def load_w2(s, g, v2, cc):
                wait(sp, conv2_mm, s * C2 + G * g + cc - 3)
                sp.dma_start(w2t[0:64, cc, :], band2_d[:, v2, bass.ds(g * G + cc, 1), :].rearrange("i c z -> i (c z)")
                             ).then_inc(w2_loaded[cc], 16)

            def load_phases(s, g, h, q):
                wait(sp, conv2_mm, s * C2 + G * g - G)
                sp.wait_ge(att1_stored[q], 64 * (s * 8 + h + 1))
                for r in range(NPH):
                    for i0, n in ((0, 48), (48, 6 if r == 0 else 5)):
                        src = bass.AP(att_d.tensor, s * (C * CHS) + g * (G * CHS) + (i0 * NPH + r) * W,
                                      [[NPH * W, n], [CHS, G], [1, W]])
                        sp.dma_start(ph[i0:i0 + n, q, :, r, PADL:PADL + W], src).then_inc(ph_loaded[q], 16)

            def load_chunk(sd, g, cp):
                n = sd * NG + g
                wait_alone(sp, gate_stored, 48 * (sd + 1))
                wait(sp, out_stored[cp], 16 * n)
                px = bass.ds((2 * g + cp) * CHUNK, CHUNK)
                xf = x[sd].rearrange("c h w -> c (h w)")
                sp.dma_start(dx[:, cp, :], xf[:, px]).then_inc(d_loaded[cp], 16)
                sp.dma_start(da[:, cp, :], att_d[sd, :, px]).then_inc(d_loaded[cp], 16)
                sp.dma_start(gt[:, cp, :], gate_d[sd, :, px]).then_inc(d_loaded[cp], 16)

            def exchange_maps(s):
                store_maps(sp, s, 0)
                if isinstance(s, int) and s == 0:
                    sp.wait_ge(s_mapzero, 32)
                for m in range(2):
                    wait_alone(sp, maps_stored[m], 80 * (s + 1))
                wait_alone(sp, sp_mm, 2 * s)
                for m in range(2):
                    for k, t in enumerate((mina[:, :, 3:3 + W], minb)):
                        src = bass.AP(map_d.tensor, s * (4 * 168 * W) + (2 * k + m) * 168 * W,
                                      [[W, 48], [SPB * W, 4], [1, W]])
                        sp.dma_start(t[64 * m:64 * m + 48, :, :], src).then_inc(min_loaded, 16)

            for b in range(2):
                load_x(0, b)
            sp.wait_ge(s_pad_d, 48)
            def expand(band, pad, rows, n, width):
                sp.dma_start(bass.AP(band.tensor, 0, [[width, n], [n * width, rows], [1, width]]),
                             bass.AP(pad.tensor, width - 1, [[2 * width, n], [-1, rows], [1, width]])).then_inc(s_band, 16)

            expand(band1_d, pad1_d, RIN1, 2 * C2 * J1, 32)
            expand(bandsp_d, padsp_d, 48, 28, 64)
            sp.wait_ge(s_band, 32)
            sp.wait_ge(s_init, 1)
            for i in range(2):
                sp.dma_start(wsp[64 * i:64 * i + 48, :, :].rearrange("p k (o z) -> p (k o) z", o=2),
                             bandsp_d[:, 14 * i:14 * i + 14, :]).then_inc(s_wsp, 16)
            expand(band2_d, pad2_d, 64, 3 * C2 * J2, 64)
            for b in range(2, NB1):
                load_x(0, b)
            sp.wait_ge(s_band, 48)

            def sample(s, first, last):
                wait_alone(sp, idx_ready, s + 1)
                v1 = sp.value_load(idx[0:1, 0:1], min_val=0, max_val=1)
                v2 = sp.value_load(idx[0:1, 1:2], min_val=0, max_val=2)
                load_w1(s, 0, v1, 0)
                load_w1(s, 1, v1, 1)
                wait_alone(sp, conv1_evac, 32 * s)
                wait_alone(sp, acc1_steps, MAP_STEPS * s)
                wait_alone(sp, conv2_evac, 32 * s)
                wait_alone(sp, acc2_steps, MAP_STEPS * s)
                if first:
                    sp.wait_ge(s_wnat, 16 * 19)
                for t, v in ((bias1, v1 * C2), (bias2, v2 * C2 + 2 * C2)):
                    sp.dma_start(t[:, :], bass.AP(bias_d.tensor, v, [[0, 128], [1, C2]])).then_inc(bias_loaded, 16)
                if not first:
                    exchange_maps(s - 1)
                load_phases(s, 0, 0, 0)
                if not first:
                    for q in range(2):
                        wait_alone(sp, att1_stored[q], 512 * s)
                        wait_alone(sp, att2_stored[q], 512 * s)

                def conv2_loads(g, h, q, last_group=False):
                    load_w2(s, g, v2, 0)
                    load_w2(s, g, v2, 1)
                    load_w2(s, g, v2, 2)
                    if not first:
                        load_chunk(s - 1, g, 0)
                    if not last_group:
                        load_phases(s, g + 1, h + q, 1 - q)
                    load_w2(s, g, v2, 3)
                    if not first:
                        load_chunk(s - 1, g, 1)

                def groups(h):
                    for q in range(2):
                        load_w1(s, 2 * h + 2 + q, v1, q)
                        conv2_loads(2 * h + q, h, q)

                repeat(sp, 0, 3, groups, peel(s))
                if not last:
                    load_x(s + 1, 0)
                repeat(sp, 3, 5, groups)
                if not last:
                    load_x(s + 1, 1)
                repeat(sp, 5, 7, groups)

                conv2_loads(14, 7, 0)
                if not last:
                    for b in range(2, NB1):
                        load_x(s + 1, b)
                conv2_loads(15, 7, 1, last_group=True)
                if last:
                    exchange_maps(s)

            samples(sp, sample)
            for q in range(2):
                sp.wait_ge(att1_stored[q], 512 * B)
                sp.wait_ge(att2_stored[q], 512 * B)

            def last_chunks(g):
                for cp in range(2):
                    load_chunk(B - 1, g, cp)
            repeat(sp, 0, NG, last_chunks)

        @block.gpsimd
        def _(pool):
            nc.gpsimd.memset(xpf[0:C2, 0:oS], 0.0).then_inc(s_padzero, 1)
            nc.gpsimd.memset(xs[:, 0, 0:2, :], 0.0).then_inc(x_zeroed, 1)
            nc.gpsimd.memset(st1[0:4 * B, 0, :], 0.0)
            nc.gpsimd.memset(wsp[:, :, :], 0.0)
            nc.gpsimd.memset(mina[:, :, :], 0.0)
            nc.gpsimd.memset(ones3[:, :], 1.0)
            nc.gpsimd.memset(ph[:, :, :, :, :], 0.0).then_inc(s_init, 1)
            pool.wait_ge(s_init, 1)
            md = map_d.rearrange("b m h w -> (b m) (h w)")
            pool.dma_start(md[:, 0:3 * W], st1[0:4 * B, 0, 0:3 * W]).then_inc(s_mapzero, 16)
            pool.dma_start(md[:, 163 * W:168 * W], st1[0:4 * B, 0, 0:5 * W]).then_inc(s_mapzero, 16)

            def zero_rows(s, b):
                jb = s * NB1 + b
                wait_alone(pool, xr_ready, 2 * (jb - 1))
                rows = slice(0, 2) if b == 0 else slice(H - (ROUT1 * b - 2), RIN1)
                nc.gpsimd.memset(xs[:, b % 2, rows, :], 0.0).then_inc(x_zeroed, 1)

            zero_rows(0, NB1 - 1)

            def store_chunk(sd, g, cp):
                ci = (sd * NG + g) * 2 + cp
                pool.wait_ge(d_done, 2 * ci + 2)
                of = out[sd].rearrange("c h w -> c (h w)")
                pool.dma_start(of[:, bass.ds((2 * g + cp) * CHUNK, CHUNK)], dx[:, cp, :]).then_inc(out_stored[cp], 16)

            def store_gate(s):
                pool.wait_ge(gate_steps, 6 * (s + 1))
                for k in range(3):
                    d = gate_d[s, k, :].rearrange("(b i w) -> i b w", i=SPB, w=W)
                    pool.dma_start(d, gparts[:, k, :].rearrange("p (b w) -> p b w", w=W)).then_inc(gate_stored, 16)

            def store_att2(s, g, q):
                pool.wait_ge(conv2_evac, s * 32 + 2 * g + 2)
                for ch in range(2):
                    for i0, n in ((0, 48), (48, 6)):
                        d = bass.AP(att_d.tensor, s * (C * CHS) + (g * G + C2 + ch) * CHS + i0 * NPH * W,
                                    [[NPH * W, n], [2 * CHS, 2], [1, NPH * W]])
                        pool.dma_start(d, st2[64 * ch + i0:64 * ch + i0 + n, q, :, :]).then_inc(att2_stored[q], 16)

            def sample(s, first, last):
                def group_stores(g, q):
                    if not first:
                        store_chunk(s - 1, g, 0)
                        store_chunk(s - 1, g, 1)
                    store_att2(s, g, q)

                def groups(h):
                    for q in range(2):
                        group_stores(2 * h + q, q)
                if not first:
                    store_gate(s - 1)
                repeat(pool, 0, 3, groups, peel(s))
                if not last:
                    zero_rows(s + 1, 0)
                repeat(pool, 3, 7, groups)
                if not last:
                    zero_rows(s + 1, NB1 - 1)
                for q in range(2):
                    group_stores(14 + q, q)
                store_maps(pool, s, 1)
                if last:
                    store_gate(s)

            samples(pool, sample)

            def last_chunks(g):
                for cp in range(2):
                    store_chunk(B - 1, g, cp)
            repeat(pool, 0, NG, last_chunks)
            for cp in range(2):
                pool.wait_ge(out_stored[cp], 16 * NG * B)
            pool.wait_ge(s_band, 48)
            pool.wait_ge(gate_stored, 48 * B)
            for q in range(2):
                pool.wait_ge(att1_stored[q], 512 * B)
                pool.wait_ge(att2_stored[q], 512 * B)

        @block.scalar
        def _(act):
            act.wait_ge(s_pad, 3)
            act.dma_start(pad1_d.rearrange("(v c j) z -> c v (j z)", v=2, c=C2),
                          pad1.rearrange("p v j z -> p v (j z)")).then_inc(s_pad_d, 16)
            act.dma_start(padsp_d.rearrange("(a r) z -> a r z", a=1), padsp).then_inc(s_pad_d, 16)
            act.dma_start(pad2_d.rearrange("(v c j) z -> c v (j z)", v=3, c=C2),
                          pad2.rearrange("p v j z -> p v (j z)")).then_inc(s_pad_d, 16)
            act.wait_ge(s_pad_d, 48)

            def evac_proj(s, b2):
                for bb in range(2):
                    b = 2 * b2 + bb
                    for k, (t0, t1) in enumerate(FILLS):
                        n = (s * NB1 + b) * NF + k
                        act.wait_ge(proj_mm, n + 1)
                        dst = xp[:, :, b, t0:t1].rearrange("p c t -> p t c")
                        src = psP[k % 2][:, 0:64 * (t1 - t0)].rearrange("p (t c) -> p t c", c=C2)
                        nc.scalar.activation(dst, src, ACT.Identity).then_inc(proj_evac, 1)

            def evac_conv1(s, g, h, q):
                wait(act, att1_stored[q], 64 * (s * 8 + h))
                for pr in range(2):
                    P = s * 32 + 2 * g + pr
                    act.wait_ge(conv1_mm, P + 1)
                    for ch in range(2):
                        cc = 2 * pr + ch
                        ps = ps1[pr][:, ch * N1:(ch + 1) * N1].rearrange("p (b t) -> p b t", t=TO1)
                        dst = st1[32 * cc:32 * cc + ROUT1, q, :].rearrange("p (b t k) -> p b t k", b=NB1, k=Q1)
                        for k in range(Q1):
                            t0 = 1 if k < 2 else 0
                            ins = nc.scalar.activation(dst[:, :, :, (k + 2) % 4], ps[32 * k:32 * k + ROUT1, :, t0:t0 + T1],
                                                       ACT.Identity, bias=bias1[32 * k:32 * k + ROUT1, bass.ds(g * G + cc, 1)])
                    ins.then_inc(conv1_evac, 1)
                act.wait_ge(conv1_evac, s * 32 + 2 * g + 2)
                for cc in range(G):
                    d = att_d[s, g * G + cc, :].rearrange("(b i w) -> i b w", i=ROUT1, w=W)
                    act.dma_start(d, st1[32 * cc:32 * cc + ROUT1, q, :].rearrange("p (b w) -> p b w", w=W)
                                  ).then_inc(att1_stored[q], 16)

            def evac_conv2(s, g, h, q, last_group=False):
                copy_w2(s, g, 3)
                wait(act, att2_stored[q], 64 * (s * 8 + h))
                for pr in range(2):
                    act.wait_ge(conv2_mm, s * C2 + G * g + 2 * pr + 2)
                    for ch in range(2):
                        ps = ps2[pr][:, ch * N2:(ch + 1) * N2].rearrange("p (r t) -> p r t", t=PO2)
                        dst = st2[64 * ch:64 * ch + RPH, q, pr, :].rearrange("p (r t k) -> p r t k", r=NPH, k=2)
                        for k in range(2):
                            p0 = 2 if k == 0 else 0
                            ins = nc.scalar.activation(dst[:, :, :, 1 - k], ps[64 * k:64 * k + RPH, :, p0:p0 + 80],
                                                       ACT.Identity, bias=bias2[64 * k:64 * k + RPH, bass.ds(g * G + 2 * pr + ch, 1)])
                    ins.then_inc(conv2_evac, 1)
                    if pr == 0 and not last_group:
                        copy_w2(s, g + 1, 0)
                        copy_w2(s, g + 1, 1)
                if not last_group:
                    copy_w2(s, g + 1, 2)

            def copy_w2(s, g, cc):
                act.wait_ge(w2_loaded[cc], 16 * (s * NG + g + 1))
                nc.scalar.copy(w2t[64:64 + RPH, cc, 64:WB2], w2t[0:RPH, cc, 0:WB2 - 64]).then_inc(w2_copied, 1)

            def sigmoids(s):
                for hf in range(2):
                    act.wait_ge(sp_mm, 2 * s + hf + 1)
                    if hf == 0:
                        wait(act, gate_steps, 6 * s)
                    for o in range(2):
                        ins = nc.scalar.activation(sg[:, o, 320 * hf:320 * hf + 320], psP[hf][64 * o:64 * o + SPB, 0:320],
                                                   ACT.Sigmoid, bias=spbt[64 * o:64 * o + SPB, o:o + 1])
                    ins.then_inc(sig_done, 1)

            repeat(act, 0, 3, lambda b2: evac_proj(0, b2))
            act.wait_ge(s_mapzero, 32)

            def sample(s, first, last):
                act.wait_ge(bias_loaded, 32 * (s + 1))
                evac_conv1(s, 0, 0, 0)
                evac_conv1(s, 1, 0, 1)
                if not first:
                    sigmoids(s - 1)
                copy_w2(s, 0, 0)
                copy_w2(s, 0, 1)
                copy_w2(s, 0, 2)

                def groups(h):
                    for q in range(2):
                        evac_conv1(s, 2 * h + 2 + q, h + 1, q)
                        evac_conv2(s, 2 * h + q, h, q)
                repeat(act, 0, 7, groups, peel(s))
                if not last:
                    act.wait_ge(conv1_mm, 32 * (s + 1))
                    repeat(act, 0, 3, lambda b2: evac_proj(s + 1, b2))
                for q in range(2):
                    evac_conv2(s, 14 + q, 7, q, last_group=(q == 1))
                if last:
                    sigmoids(s)

            samples(act, sample)
            for q in range(2):
                act.wait_ge(att1_stored[q], 512 * B)
                act.wait_ge(att2_stored[q], 512 * B)

        @block.tensor
        def _(pe):
            pe.wait_ge(s_wnat, 16 * 19)

            def project(s, b2):
                for bb in range(2):
                    b = 2 * b2 + bb
                    for k, (t0, t1) in enumerate(FILLS):
                        n = (s * NB1 + b) * NF + k
                        if k % 3 == 0:
                            pe.wait_ge(xr_ready, 2 * (s * NB1 + b) + k // 3 + 1)
                        wait(pe, proj_evac, n - 1)
                        for t in range(t0, t1):
                            lhsT = xr[:, Q1 * t:Q1 * t + Q1, :].rearrange("p q i -> p (q i)")
                            ins = nc.tensor.matmul(psP[k % 2][:, 64 * (t - t0):64 * (t - t0) + 64], lhsT, projt[:, :],
                                                   start=True, stop=True)
                        ins.then_inc(proj_mm, 1)

            def project_all(s):
                repeat(pe, 0, 3, lambda b2: project(s, b2), 1 if isinstance(s, int) and s == 0 else 0)

            def route_stats(s):
                pe.wait_ge(stats_ready, s + 1)
                pe.wait_ge(proj_evac, NB1 * NF * (s + 1))
                nc.tensor.matmul(psP[0][0:C2, 0:25], projt[:, :], stats[:, :, :].rearrange("p r c -> p (r c)"),
                                 start=True, stop=True).then_inc(stats_mm, 1)

            def route_logits(s):
                wait_alone(pe, pool_ready, s + 1)
                for n, (o, m, rhs) in enumerate(((32, 2, a1t), (40, 3, a2t), (48, 3, a2t))):
                    ins = nc.tensor.matmul(psP[0][0:1, o:o + m], pooled[:, n:n + 1], rhs[:, :], start=True, stop=True)
                ins.then_inc(logits_mm, 1)

            def spatial(s):
                pe.wait_ge(min_steps, 3 * (s + 1))
                for hf in range(2):
                    for kw in range(7):
                        ins = nc.tensor.matmul(psP[hf][0:104, 0:320], wsp[0:112, kw, 0:104], mina[0:112, 2 * hf:2 * hf + 2, kw:kw + W],
                                               start=(kw == 0), stop=(kw == 6))
                    ins.then_inc(sp_mm, 1)

            def conv1(s, g, h, q):
                pe.wait_ge(w1_loaded[q], 64 * (s * 8 + h + 1))
                for pr in range(2):
                    wait(pe, acc1_steps, s * MAP_STEPS + 2 + 4 * (2 * g + pr - 1))
                    for ch in range(2):
                        cc = 2 * pr + ch
                        o = ps1[pr][:, ch * N1:(ch + 1) * N1].rearrange("p (b t) -> p b t", t=TO1)
                        rhs = xp[:, bass.ds(g * G + cc, 1), :, :].rearrange("p c b t -> p (c b) t")
                        nc.tensor.matmul(o[:, :, 0:T1], w1t[:, q, cc, 0:128], rhs, start=True, stop=False, skip_group_check=True)
                        ins = nc.tensor.matmul(o[:, :, 1:1 + T1], w1t[:, q, cc, 128:256], rhs, start=False, stop=True,
                                               skip_group_check=True)
                    ins.then_inc(conv1_mm, 1)

            def conv2(s, g, h, q, pr):
                if pr == 0:
                    pe.wait_ge(ph_loaded[q], 96 * (s * 8 + h + 1))
                    pe.wait_ge(ph_copied, s * NG + g + 1)
                wait(pe, acc2_steps, s * MAP_STEPS + 2 + 4 * (2 * g + pr - 1))
                for ch in range(2):
                    cc = 2 * pr + ch
                    pe.wait_ge(w2_loaded[cc], 16 * (s * NG + g + 1))
                    pe.wait_ge(w2_copied, s * C2 + G * g + cc + 1)
                    o = ps2[pr][0:118, ch * N2:(ch + 1) * N2].rearrange("p (r t) -> p r t", t=PO2)
                    for d in SHIFTS2:
                        lo, hi = RANGE2[d]
                        f = PADL + 2 * lo + 6 * d
                        ins = nc.tensor.matmul(o[:, :, lo:hi], w2t[0:118, cc, (5 - 2 * d) * 64:(5 - 2 * d) * 64 + 118],
                                               ph[0:118, q, cc, :, f:f + 2 * (hi - lo) - 1:2],
                                               start=(d == 0), stop=(d == SHIFTS2[-1]), skip_group_check=True)
                    ins.then_inc(conv2_mm, 1)

            def broadcast(sd, g, cp):
                ci = (sd * NG + g) * 2 + cp
                pe.wait_ge(d_loaded[cp], 48 * (sd * NG + g + 1))
                wait(pe, d_done, 2 * ci)
                for sub in range(2):
                    nc.tensor.matmul(psG[sub][:, 0:SUB], ones3[:, :], gt[:, cp, sub * SUB:(sub + 1) * SUB],
                                     start=True, stop=True).then_inc(d_bc, 1)

            project_all(0)
            route_stats(0)
            route_logits(0)

            def sample(s, first, last):
                if first:
                    pe.wait_ge(s_init, 1)
                    pe.wait_ge(s_wsp, 32)
                conv1(s, 0, 0, 0)
                conv1(s, 1, 0, 1)
                if not first:
                    pe.wait_ge(idx_ready, s + 1)
                    spatial(s - 1)

                def group(g, h, q, between=None):
                    for pr in range(2):
                        if not first:
                            broadcast(s - 1, g, pr)
                        if pr == 1 and between is not None:
                            between(s + 1)
                        conv2(s, g, h, q, pr)

                def groups(h):
                    for q in range(2):
                        conv1(s, 2 * h + q + 2, h + 1, q)
                        group(2 * h + q, h, q)
                repeat(pe, 0, 7, groups, peel(s))
                if not last:
                    wait_alone(pe, sig_done, 2 * s)
                    project_all(s + 1)
                group(14, 7, 0, between=None if last else route_stats)
                group(15, 7, 1, between=None if last else route_logits)
                if last:
                    wait(pe, sig_done, 2 * s)
                    spatial(s)

            samples(pe, sample)

            def last_chunks(g):
                for cp in range(2):
                    broadcast(B - 1, g, cp)
            repeat(pe, 0, NG, last_chunks)

        @block.vector
        def _(dve):
            dve.wait_ge(s_padzero, 1)
            dve.wait_ge(s_wnat, 16 * 19)
            o = 0
            for dst, ks, kmax, z0, jn in ((pad1, K1, 5, 31, 7), (pad2, K2, 11, 68, 11)):
                for v, k in enumerate(ks):
                    e = (kmax - k) // 2
                    for kh in range(k):
                        src = wnat[:, o + kh * k + k - 1:o + kh * k + k]
                        ins = nc.vector.tensor_copy(dst[:, v, jn - e - (k - 1):jn - e + 1, z0 - e - kh], neg_step(src, k))
                    o += k * k
                ins.then_inc(s_pad, 1)
            for kh in range(7):
                for i in range(2):
                    ins = nc.vector.tensor_copy(
                        padsp[:, 14 * i:14 * i + 14, 63 - kh].rearrange("p (k o) -> p o k", o=2),
                        spw[:, :].rearrange("p (o i h w) -> p o i h w", o=2, i=2, h=7)[:, :, i, kh, :])
            ins.then_inc(s_pad, 1)

            def take_x(s, b):
                q, jb = b % 2, s * NB1 + b
                dve.wait_ge(x_loaded[q], 16 * (3 * s + b // 2 + 1))
                own = slice(2, 2 + (ROUT1 if b < NB1 - 1 else H - ROUT1 * (NB1 - 1)))
                if b == 0 or b == NB1 - 1:
                    dve.wait_ge(x_zeroed, 2 * s + (1 if b == 0 else 2))
                    r0, i0 = (1, 2) if b == 0 else (3, 20)
                    nc.vector.tensor_reduce(stats[:, r0:r0 + 2, 0], xs[:, q, i0:i0 + 2, :], AX.X, ALU.add)
                    nc.vector.tensor_copy(stats[:, r0:r0 + 2, 1:3], xs[:, q, i0:i0 + 2, 0:2])
                    nc.vector.tensor_copy(stats[:, r0:r0 + 2, 3:5], xs[:, q, i0:i0 + 2, W - 2:W])
                nc.vector.tensor_reduce(part[:, b, 2:4], xs[:, q, own, 0:2].rearrange("p i w -> p w i"), AX.X, ALU.add)
                nc.vector.tensor_reduce(part[:, b, 4:6], xs[:, q, own, W - 2:W].rearrange("p i w -> p w i"), AX.X, ALU.add)
                for hf in range(2):
                    wait(dve, proj_mm, NF * (jb - 1) + 3 * hf + 3)
                    w = slice(hf * 80, hf * 80 + 80)
                    dst = xr[:, w, :].rearrange("p w i -> p i w")
                    nc.vector.tensor_scalar(dst[:, own, :], xs[:, q, own, w], 1.0, None, ALU.mult, ALU.add,
                                            accum_out=part[:, b, hf:hf + 1])
                    if own.stop < ROUT1 + 2:
                        nc.vector.tensor_copy(dst[:, own.stop:ROUT1 + 2, :], xs[:, q, own.stop:ROUT1 + 2, w])
                    nc.vector.tensor_copy(dst[:, 0:2, :], xs[:, q, 0:2, w])
                    nc.vector.tensor_copy(dst[:, ROUT1 + 2:, :], xs[:, q, ROUT1 + 2:, w]).then_inc(xr_ready, 1)

            def stats_total(s):
                dve.wait_ge(xr_ready, 2 * NB1 * (s + 1))
                nc.vector.tensor_reduce(stats[:, 0, 1:5], part[:, :, 2:6].rearrange("p b k -> p k b"), AX.X, ALU.add)
                nc.vector.tensor_reduce(stats[:, 0, 0:1], part[:, :, 0:2], AX.XY, ALU.add).then_inc(stats_ready, 1)

            def stepper(s, n):
                def step(ins):
                    n[0] += 1
                    ins.then_inc(route_steps, 1)
                    dve.wait_ge(route_steps, s * ROUTE_STEPS + n[0])
                return step

            def route_means(s):
                n = [0]
                step = stepper(s, n)
                dve.wait_ge(stats_mm, s + 1)
                step(nc.vector.tensor_copy(psx[:, :, :].rearrange("p r c -> p (r c)"), psP[0][0:C2, 0:25]))
                for dst, src, ax in ((srow, psx, 0), (swin, srow, 1)):
                    def line(t, k):
                        return t[:, k, :] if ax == 0 else t[:, :, k]
                    step(nc.vector.tensor_copy(line(dst, 2), line(src, 0)))
                    step(nc.vector.tensor_tensor(line(dst, 1), line(src, 0), line(src, 4), ALU.subtract))
                    step(nc.vector.tensor_tensor(line(dst, 0), line(dst, 1), line(src, 3), ALU.subtract))
                    step(nc.vector.tensor_tensor(line(dst, 3), line(src, 0), line(src, 1), ALU.subtract))
                    step(nc.vector.tensor_tensor(line(dst, 4), line(dst, 3), line(src, 2), ALU.subtract))
                step(nc.vector.tensor_tensor(wmul[:, 0:9].rearrange("p (a b) -> p a b", a=3),
                                             wnat[:, 0:9].rearrange("p (a b) -> p a b", a=3), swin[:, 1:4, 1:4], ALU.mult))
                step(nc.vector.tensor_tensor(wmul[:, 9:34], wnat[:, 9:34], swin[:, :, :].rearrange("p a b -> p (a b)"), ALU.mult))
                step(nc.vector.tensor_reduce(pooled[:, 1:2], wmul[:, 0:9], AX.X, ALU.add))
                step(nc.vector.tensor_reduce(pooled[:, 2:3], wmul[:, 9:34], AX.X, ALU.add))
                step(nc.vector.tensor_scalar(pooled[:, 1:3], pooled[:, 1:3], 1.0 / PIX, None, ALU.mult))
                step(nc.vector.tensor_tensor(pooled[:, 1:3], pooled[:, 1:3], b1n[:, :], ALU.add))
                nc.vector.tensor_scalar(pooled[:, 0:1], psx[:, 0, 0:1], 1.0 / PIX, None, ALU.mult).then_inc(pool_ready, 1)
                assert n[0] == MEAN_STEPS

            def route_indices(s):
                n = [MEAN_STEPS]
                step = stepper(s, n)
                dve.wait_ge(logits_mm, s + 1)
                step(nc.vector.tensor_tensor(lg[:, 0:2], psP[0][0:1, 32:34], attb[:, 0:2], ALU.add))
                step(nc.vector.tensor_tensor(lg[:, 2:5], psP[0][0:1, 40:43], attb[:, 2:5], ALU.add))
                step(nc.vector.tensor_tensor(lg[:, 5:8], psP[0][0:1, 48:51], attb[:, 2:5], ALU.add))
                l2 = lg[:, 2:8].rearrange("p (v k) -> p v k", k=3)
                step(nc.vector.tensor_tensor(lg[:, 8:9], lg[:, 1:2], lg[:, 0:1], ALU.is_gt))
                step(nc.vector.tensor_tensor(lg[:, 10:12], l2[:, :, 1], l2[:, :, 0], ALU.is_gt))
                step(nc.vector.tensor_tensor(lg[:, 12:14], l2[:, :, 1], l2[:, :, 0], ALU.max))
                step(nc.vector.tensor_tensor(lg[:, 14:16], l2[:, :, 2], lg[:, 12:14], ALU.is_gt))
                step(nc.vector.tensor_scalar(lg[:, 16:18], lg[:, 10:12], -1.0, 2.0, ALU.mult, ALU.add))
                step(nc.vector.tensor_tensor(lg[:, 18:20], lg[:, 16:18], lg[:, 14:16], ALU.mult))
                step(nc.vector.tensor_tensor(lg[:, 20:22], lg[:, 18:20], lg[:, 10:12], ALU.add))
                step(nc.vector.tensor_tensor(lg[:, 22:23], lg[:, 21:22], lg[:, 20:21], ALU.subtract))
                step(nc.vector.tensor_tensor(lg[:, 23:24], lg[:, 22:23], lg[:, 8:9], ALU.mult))
                step(nc.vector.tensor_tensor(lg[:, 9:10], lg[:, 23:24], lg[:, 20:21], ALU.add))
                wait(dve, bias_loaded, 32 * s)
                nc.vector.tensor_copy(idx[:, :], lg[:, 8:10]).then_inc(idx_ready, 1)
                assert n[0] == ROUTE_STEPS

            def init_maps(s):
                if not (isinstance(s, int) and s == 0):
                    dve.wait_ge(nat_ready, s)
                for a, steps in ((acc1, acc1_steps), (acc2, acc2_steps)):
                    nc.vector.memset(a[:, 0, :], 0.0).then_inc(steps, 1)
                    nc.vector.memset(a[:, 1, :], NEG).then_inc(steps, 1)

            def update_maps(s, g, pr, which):
                a, bias, ps, n, lanes, steps, evac = (
                    (acc1, bias1, ps1, N1, 128, acc1_steps, conv1_evac) if which == 1 else
                    (acc2, bias2, ps2, N2, 118, acc2_steps, conv2_evac))
                dve.wait_ge(evac, s * 32 + 2 * g + pr + 1)
                for ch in range(2):
                    src = ps[pr][0:lanes, ch * n:(ch + 1) * n]
                    bb = bias[0:lanes, bass.ds(g * G + 2 * pr + ch, 1)]
                    for m, op in ((0, ALU.add), (1, ALU.max)):
                        k = 2 + 2 * ch + m
                        dve.wait_ge(steps, s * MAP_STEPS + 4 * (2 * g + pr) + k - 1)
                        nc.vector.scalar_tensor_tensor(out=a[0:lanes, m, :], in0=src, scalar=bb, in1=a[0:lanes, m, :],
                                                       op0=ALU.add, op1=op).then_inc(steps, 1)

            def gate_chunk(sd, g, cp):
                ci = (sd * NG + g) * 2 + cp
                dve.wait_ge(d_loaded[cp], 48 * (sd * NG + g + 1))
                for sub in range(2):
                    px = slice(sub * SUB, (sub + 1) * SUB)
                    dve.wait_ge(d_bc, 2 * ci + sub + 1)
                    nc.vector.tensor_tensor(psG[sub][:, 0:SUB], psG[sub][:, 0:SUB], da[:, cp, px], ALU.mult).then_inc(d_mul, 1)
                for sub in range(2):
                    px = slice(sub * SUB, (sub + 1) * SUB)
                    dve.wait_ge(d_mul, 2 * ci + sub + 1)
                    nc.vector.tensor_tensor(dx[:, cp, px], psG[sub][:, 0:SUB], dx[:, cp, px], ALU.add).then_inc(d_done, 1)

            def copy_out_maps(s):
                dve.wait_ge(acc1_steps, MAP_STEPS * (s + 1))
                dve.wait_ge(acc2_steps, MAP_STEPS * (s + 1))
                for m in range(2):
                    wait(dve, maps_stored[m], 80 * s)
                for m in range(2):
                    a = acc1[:, m, :].rearrange("p (b t) -> p b t", t=TO1)
                    d = nat1[32 * m:32 * m + ROUT1, :].rearrange("p (b t k) -> p b t k", b=NB1, k=Q1)
                    for k in range(Q1):
                        t0 = 1 if k < 2 else 0
                        nc.vector.tensor_copy(d[:, :, :, (k + 2) % 4], a[32 * k:32 * k + ROUT1, :, t0:t0 + T1])
                    a = acc2[:, m, :].rearrange("p (r t) -> p r t", t=PO2)
                    d = nat2[64 * m:64 * m + RPH, :].rearrange("p (r t k) -> p r t k", r=NPH, k=2)
                    for k in range(2):
                        p0 = 2 if k == 0 else 0
                        ins = nc.vector.tensor_copy(d[:, :, :, 1 - k], a[64 * k:64 * k + RPH, :, p0:p0 + 80])
                ins.then_inc(nat_ready, 1)

            def combine_maps(s):
                dve.wait_ge(min_loaded, 64 * (s + 1))
                px = slice(3, 3 + W)
                nc.vector.tensor_tensor(mina[64:112, :, px], mina[64:112, :, px], minb[64:112, :, :], ALU.max).then_inc(min_steps, 1)
                nc.vector.tensor_tensor(mina[0:48, :, px], mina[0:48, :, px], minb[0:48, :, :], ALU.add).then_inc(min_steps, 1)
                dve.wait_ge(min_steps, 3 * s + 2)
                nc.vector.tensor_scalar(mina[0:48, :, px], mina[0:48, :, px], 1.0 / C, None, ALU.mult).then_inc(min_steps, 1)

            def gate(s):
                dve.wait_ge(sig_done, 2 * (s + 1))
                wait(dve, gate_stored, 48 * s)
                nc.vector.tensor_tensor(sg[:, 0, :], sg[:, 0, :], sg[:, 1, :], ALU.add).then_inc(gate_steps, 1)
                for k in range(3):
                    dve.wait_ge(gate_steps, 6 * s + 2 * k + 1)
                    nc.vector.tensor_copy(gparts[:, k, :], sg[:, k % 2, :]).then_inc(gate_steps, 1)
                    if k < 2:
                        dve.wait_ge(gate_steps, 6 * s + 2 * k + 2)
                        nc.vector.tensor_tensor(sg[:, 1 - k % 2, :], sg[:, k % 2, :], gparts[:, k, :],
                                                ALU.subtract).then_inc(gate_steps, 1)

            def copy_phases(s, g, h, q):
                dve.wait_ge(ph_loaded[q], 96 * (s * 8 + h + 1))
                nc.vector.tensor_copy(ph[64:64 + RPH, q, :, :, 0:W].rearrange("p c r w -> p (c r) w"),
                                      ph[0:RPH, q, :, :, PADL:PADL + W].rearrange("p c r w -> p (c r) w")
                                      ).then_inc(ph_copied, 1)

            for b in range(NB1):
                take_x(0, b)
            stats_total(0)
            route_means(0)
            route_indices(0)

            def sample(s, first, last):
                init_maps(s)
                dve.wait_ge(bias_loaded, 32 * (s + 1))
                for g in range(2):
                    for pr in range(2):
                        update_maps(s, g, pr, 1)
                if not first:
                    combine_maps(s - 1)
                    gate(s - 1)
                copy_phases(s, 0, 0, 0)

                def group(g, h, q, conv1_too=True, last_group=False, between=None):
                    if not first:
                        gate_chunk(s - 1, g, 0)
                    if conv1_too:
                        for pr in range(2):
                            update_maps(s, g + 2, pr, 1)
                    if not first:
                        gate_chunk(s - 1, g, 1)
                    update_maps(s, g, 0, 2)
                    if not last_group:
                        copy_phases(s, g + 1, h + q, 1 - q)
                    if between is not None:
                        between(s + 1)
                    update_maps(s, g, 1, 2)

                def groups(h):
                    for q in range(2):
                        group(2 * h + q, h, q)
                repeat(dve, 0, 3, groups, peel(s))
                if not last:
                    take_x(s + 1, 0)
                repeat(dve, 3, 7, groups)
                if not last:
                    for b in range(1, NB1):
                        take_x(s + 1, b)
                    stats_total(s + 1)
                group(14, 7, 0, conv1_too=False, between=None if last else route_means)
                group(15, 7, 1, conv1_too=False, last_group=True, between=None if last else route_indices)
                copy_out_maps(s)
                if last:
                    combine_maps(s)
                    gate(s)

            samples(dve, sample)

            def last_chunks(g):
                for cp in range(2):
                    gate_chunk(B - 1, g, cp)
            repeat(dve, 0, NG, last_chunks)


_INS = ['x', 'L0_conv_proj_w', 'L0_conv_dw1_w3', 'L0_conv_dw1_b3', 'L0_conv_dw1_w5', 'L0_conv_dw1_b5',
        'L0_conv_dw2_w7', 'L0_conv_dw2_b7', 'L0_conv_dw2_w9', 'L0_conv_dw2_b9', 'L0_conv_dw2_w11', 'L0_conv_dw2_b11',
        'L0_conv_att1_w', 'L0_conv_att1_b', 'L0_conv_att2_w', 'L0_conv_att2_b', 'L0_conv_sp_w', 'L0_conv_sp_b']


def kernel(**inputs):
    import numpy as _np
    import concourse.bacc as _bacc
    from concourse import mybir as _mybir
    from concourse.bass_utils import run_bass_kernel_spmd as _run

    nc = _bacc.Bacc("TRN2", target_bir_lowering=False, num_devices=1)
    arrays, a = {}, {}
    for name in _INS:
        v = _np.ascontiguousarray(inputs[name])
        arrays[f"in_{name}_dram"] = v
        a[name.replace("L0_conv_", "")] = nc.dram_tensor(f"in_{name}_dram", v.shape, _mybir.dt.from_np(v.dtype),
                                                         kind="ExternalInput").ap()
    x = a["x"]
    out = nc.dram_tensor("out_0_dram", tuple(inputs["x"].shape), F32, kind="ExternalOutput").ap()
    conv_block(nc, x, a["proj_w"], [a["dw1_w3"], a["dw1_w5"]], [a["dw1_b3"], a["dw1_b5"]],
               [a["dw2_w7"], a["dw2_w9"], a["dw2_w11"]], [a["dw2_b7"], a["dw2_b9"], a["dw2_b11"]],
               a["att1_w"], a["att1_b"], a["att2_w"], a["att2_b"], a["sp_w"], a["sp_b"], out)
    r = _run(nc, [arrays], core_ids=[0])
    return r.results[0]["out_0_dram"]
```
